# Optimizing a Trainium2 kernel written in Bass

```python
import numpy as np
import jax
import jax.numpy as jnp

def _softmax(x, axis=-1):
    return jax.nn.softmax(x, axis=axis)

def _gelu(x):
    return jax.nn.gelu(x, approximate=True)

def _silu(x):
    return jax.nn.silu(x)

def _sigmoid(x):
    return jax.nn.sigmoid(x)

def _layernorm(x, axis=-1, eps=1e-05):
    m = jnp.mean(x, axis=axis, keepdims=True)
    v = jnp.var(x, axis=axis, keepdims=True)
    return (x - m) / jnp.sqrt(v + eps)

def _scatter_add(tgt, idx, src, axis=0):
    return tgt.at[idx].add(src)

def _segment_sum(src, seg, n):
    return jax.ops.segment_sum(src, seg, n)
kernel_name = 'mk_vit_tower_d1_tok_img4096_r4_1325e6'

def setup_inputs(seed: int=0):
    np.random.seed(seed)
    _w = jnp.asarray

    def _rec_inputs():
        import jax
        import jax.numpy as jnp
        _rk = jax.random.key(seed)
        x = -0.0064186 + 0.999588 * jax.random.normal(jax.random.fold_in(_rk, 1), (16, 128, 64, 2), jnp.float32)
        return x
    x = _rec_inputs()

    def _L0_tok_setup():
        import jax, jax.numpy as jnp
        import numpy as np
        import math
        H, N, C, L_VAL = (128, 64, 1, 1024)
        EPS = 1e-07

        def _reciprocal(x, epsilon):
            xc = jnp.conj(x)
            return xc / (x * xc + epsilon)
        key = jax.random.key(seed)
        k1, k2, k3 = jax.random.split(key, 3)
        log_dt = math.log(0.001) + jax.random.uniform(k1, (H,), dtype=jnp.float32) * (math.log(0.1) - math.log(0.001))
        log_dt = jnp.tile(log_dt[:, None], (1, 2))
        lam_im = jax.random.normal(k2, (N,), dtype=jnp.float32)
        Lambda = jnp.stack([-0.5 * jnp.ones((N,), jnp.float32), lam_im], axis=-1)
        W = jax.random.normal(k3, (C, H, N, 2), dtype=jnp.float32)
        return {'log_dt': log_dt, 'Lambda': Lambda, 'W': W, 'L': L_VAL}
    _L0_tok_all = _L0_tok_setup()
    _L0_tok_in = {k: v for k, v in _L0_tok_all.items() if k in ('log_dt', 'Lambda')}
    del _L0_tok_all

    def _L0_attn_setup():
        import jax, jax.numpy as jnp
        import numpy as np
        BLOCK_H = 32
        BLOCK_W = 32
        N_FEAT = 1024
        K_FEAT = 1024
        key = jax.random.key(seed)
        k1, k2, k3 = jax.random.split(key, 3)
        data = jax.random.normal(k1, (4, 256, K_FEAT), dtype=jnp.float32)
        weight = jax.random.normal(k2, (N_FEAT, K_FEAT), dtype=jnp.float32) * 0.02
        nb, kb = (N_FEAT // BLOCK_H, K_FEAT // BLOCK_W)
        block_pattern = jax.random.randint(k3, (nb, kb), 0, 2, dtype=jnp.int32)
        mask = jnp.repeat(jnp.repeat(block_pattern, BLOCK_H, axis=0), BLOCK_W, axis=1)
        return {'data': data, 'weight': weight, 'mask': mask}
    _L0_attn_all = _L0_attn_setup()
    _L0_attn_in = {k: v for k, v in _L0_attn_all.items() if k in ('weight', 'mask')}
    del _L0_attn_all

    def _L0_ffn_setup():
        import jax, jax.numpy as jnp
        import numpy as np

        def sparsemax(z):
            E = z.shape[-1]
            z_sorted = -jnp.sort(-z, axis=-1)
            z_cum = jnp.cumsum(z_sorted, axis=-1)
            k = jnp.arange(1, E + 1, dtype=z.dtype)
            support = 1.0 + k * z_sorted > z_cum
            k_z = jnp.sum(support, axis=-1, keepdims=True)
            tau_sum = jnp.take_along_axis(z_cum, k_z.astype(jnp.int32) - 1, axis=-1)
            tau = (tau_sum - 1.0) / k_z.astype(z.dtype)
            return jnp.maximum(z - tau, 0.0)
        key = jax.random.key(seed)
        ks = jax.random.split(key, 6)
        B, S, D_IN, D_OUT, E, R = (8, 512, 1024, 1024, 8, 16)
        x = jax.random.normal(ks[0], (B, S, D_IN), dtype=jnp.float32)
        W_base = jax.random.normal(ks[1], (D_OUT, D_IN), dtype=jnp.float32) * D_IN ** (-0.5)
        b_base = jax.random.normal(ks[2], (D_OUT,), dtype=jnp.float32) * 0.01
        W_router = jax.random.normal(ks[3], (E, D_IN), dtype=jnp.float32) * D_IN ** (-0.5)
        b_router = jnp.zeros((E,), dtype=jnp.float32)
        lora_A = jax.random.normal(ks[4], (E, D_IN, R), dtype=jnp.float32) * D_IN ** (-0.5)
        lora_B = jnp.zeros((E, R, D_OUT), dtype=jnp.float32)
        return {'x': x, 'W_base': W_base, 'b_base': b_base, 'W_router': W_router, 'b_router': b_router, 'lora_A': lora_A, 'lora_B': lora_B}
    _L0_ffn_all = _L0_ffn_setup()
    _L0_ffn_in = {k: v for k, v in _L0_ffn_all.items() if k in ('W_base', 'b_base', 'W_router', 'b_router', 'lora_A', 'lora_B')}
    del _L0_ffn_all
    return {'x': x, 'L0_tok_log_dt': _L0_tok_in['log_dt'], 'L0_tok_Lambda': _L0_tok_in['Lambda'], 'L0_attn_weight': _L0_attn_in['weight'], 'L0_attn_mask': _L0_attn_in['mask'], 'L0_ffn_W_base': _L0_ffn_in['W_base'], 'L0_ffn_b_base': _L0_ffn_in['b_base'], 'L0_ffn_W_router': _L0_ffn_in['W_router'], 'L0_ffn_b_router': _L0_ffn_in['b_router'], 'L0_ffn_lora_A': _L0_ffn_in['lora_A'], 'L0_ffn_lora_B': _L0_ffn_in['lora_B']}

def reference(x, L0_tok_log_dt, L0_tok_Lambda, L0_attn_weight, L0_attn_mask, L0_ffn_W_base, L0_ffn_b_base, L0_ffn_W_router, L0_ffn_b_router, L0_ffn_lora_A, L0_ffn_lora_B):
    import jax
    import jax.numpy as jnp

    def _L0_tok_ref(log_dt, Lambda, W, L):
        import jax, jax.numpy as jnp
        import numpy as np
        import math
        H, N, C, L_VAL = (128, 64, 1, 1024)
        EPS = 1e-07

        def _reciprocal(x, epsilon):
            xc = jnp.conj(x)
            return xc / (x * xc + epsilon)
        Lam = Lambda[:, 0] + 1j * Lambda[:, 1]
        Wc = W[..., 0] + 1j * W[..., 1]
        dt = jnp.exp(log_dt)
        dt_Lambda = dt[:, None, 0] * Lambda[None, :, 0] + 1j * (dt[:, None, 1] * Lambda[None, :, 1])
        pos = jnp.arange(L, dtype=jnp.float32)
        gt0 = (Lam.real > 0).astype(dt_Lambda.real.dtype)
        P_max = jax.lax.stop_gradient(dt_Lambda * (gt0 * (L - 1)))
        dt_Lambda_neg = dt_Lambda * (1 - 2 * gt0)
        num = jnp.exp(dt_Lambda_neg) - 1
        den = jnp.exp(dt_Lambda_neg * L) - 1
        Wc = Wc * num * _reciprocal(den * Lam, EPS)
        P = dt_Lambda[..., None] * pos - P_max[..., None]
        K = jnp.einsum('chn,hnl->chl', Wc, jnp.exp(P))
        return K.real.astype(jnp.float32)

    def _L0_attn_ref(data, weight, mask):
        import jax, jax.numpy as jnp
        import numpy as np
        BLOCK_H = 32
        BLOCK_W = 32
        N_FEAT = 1024
        K_FEAT = 1024
        N, K = weight.shape
        nb, kb = (N // BLOCK_H, K // BLOCK_W)
        block_mask = mask.reshape(nb, BLOCK_H, kb, BLOCK_W).astype(jnp.float32).sum(axis=(1, 3)) > 0
        elem_mask = jnp.repeat(jnp.repeat(block_mask, BLOCK_H, axis=0), BLOCK_W, axis=1)
        w_masked = weight * elem_mask.astype(weight.dtype)
        out = jnp.einsum('bsk,nk->bsn', data, w_masked)
        return out

    def _L0_ffn_ref(x, W_base, b_base, W_router, b_router, lora_A, lora_B):
        import jax, jax.numpy as jnp
        import numpy as np

        def sparsemax(z):
            E = z.shape[-1]
            z_sorted = -jnp.sort(-z, axis=-1)
            z_cum = jnp.cumsum(z_sorted, axis=-1)
            k = jnp.arange(1, E + 1, dtype=z.dtype)
            support = 1.0 + k * z_sorted > z_cum
            k_z = jnp.sum(support, axis=-1, keepdims=True)
            tau_sum = jnp.take_along_axis(z_cum, k_z.astype(jnp.int32) - 1, axis=-1)
            tau = (tau_sum - 1.0) / k_z.astype(z.dtype)
            return jnp.maximum(z - tau, 0.0)
        base_out = jnp.einsum('bsd,od->bso', x, W_base) + b_base
        logits = jnp.einsum('bsd,ed->bse', x, W_router) + b_router
        weights = sparsemax(logits)
        h = jnp.einsum('bsd,edr->bser', x, lora_A)
        expert_out = jnp.einsum('bser,bse,ero->bso', h, weights, lora_B)
        return base_out + expert_out
    h = _L0_tok_ref(L0_tok_log_dt, L0_tok_Lambda, x, 1024)
    h = h + _L0_attn_ref(_layernorm(h, axis=-1), L0_attn_weight, L0_attn_mask)
    h = h + _L0_ffn_ref(_layernorm(h, axis=-1), L0_ffn_W_base, L0_ffn_b_base, L0_ffn_W_router, L0_ffn_b_router, L0_ffn_lora_A, L0_ffn_lora_B)
    return h

_drawn_inputs = setup_inputs


def setup_inputs(seed=0):
    import zlib

    import numpy as np

    out = dict(_drawn_inputs(seed))
    spreads = {'L0_ffn_b_router': (0.0, 0.344), 'L0_ffn_lora_B': (0.0, 0.1)}
    factors = {'L0_ffn_b_base': 6.447}
    for name, (base, spread) in spreads.items():
        noise = np.random.default_rng([zlib.crc32(name.encode()), seed]).standard_normal(out[name].shape)
        drawn = base * np.exp(spread * noise) if base else spread * noise
        out[name] = jnp.asarray(drawn.astype(out[name].dtype))
    for name, factor in factors.items():
        out[name] = (out[name] * factor).astype(out[name].dtype)
    return out
```

```python
import concourse.bass as bass
from concourse import mybir
from contextlib import ExitStack


C, H, N, L = 16, 128, 64, 1024
E, R = 8, 16
P = 128
HT = P // C
TILES = H // HT
KC = L // P
HALF = 512
NA, NB1, NB0 = 8, 8, 16
NM = NA + NB0 + NB1
SA, SB0, SB1 = slice(0, NA), slice(NA, NA + NB0), slice(NA + NB0, NM)
CAT = E * R + E
NWT = L // P
LN_EPS, REC_EPS = 1e-5, 1e-7

K_ID, K_BLK, K_MEAN, K_MUL, K_OFF, K_COL = 0, P, 2 * P, 3 * P, 3 * P + NM, 3 * P + 2 * NM
COL_G, COL_H, COL_S, COL_NS, COL_BX, COL_BY, COL_HALF, COL_BQ, COL_EPS = range(9)
K_ALL = K_COL + 9

ROUND = 12582912.0
TWO_PI = 6.28318500518798828125
INV_TWO_PI = 0.15915494309189535
LOG2E, LN2_HI, LN2_LO = 1.4426950408889634, 0.693359375, -2.12194440054690583e-4


P_ARGS = 20


def constants():
    import numpy as np

    k = np.zeros((P, K_ALL), np.float32)
    row = np.arange(P)
    k[:, K_ID:K_ID + P] = np.eye(P)
    k[:, K_BLK:K_BLK + P] = row[:, None] // 32 == row[None, :] // 32
    k[:, K_MEAN:K_MEAN + P] = 1.0 / L
    a, b0, b1 = np.arange(NA), np.arange(NB0), np.arange(NB1)
    k[:, K_MUL:K_MUL + NM] = np.concatenate([P * a, b0, NB0 * b1])
    k[:, K_OFF:K_OFF + NM] = np.concatenate(
        [np.full(NA, P * (NA - 1)), np.full(NB0, NB0 - 1), np.full(NB1, NB0 * (NB1 - 1))])
    top = row < N
    half_pi, two_pi = np.pi / 2, TWO_PI
    for col, up, down in ((COL_G, -1, 1), (COL_H, 1, -1), (COL_S, -two_pi, two_pi), (COL_NS, two_pi, -two_pi),
                          (COL_BX, half_pi, 0), (COL_BY, 0, -half_pi), (COL_HALF, half_pi, half_pi),
                          (COL_BQ, 0, half_pi), (COL_EPS, LN_EPS, LN_EPS)):
        k[:, K_COL + col] = np.where(top, up, down)
    return k


def build_vit_tower(nc, x, log_dt, lam, w_attn, mask, w_base, b_base, w_router, b_router, lora_a, lora_b,
                    consts, out):
    F, FR, I32, BF = mybir.dt.float32, mybir.dt.float32r, mybir.dt.int32, mybir.dt.bfloat16
    ALU, ACT, AX = mybir.AluOpType, mybir.ActivationFunctionType, mybir.AxisListType

    with ExitStack() as ctx:
        def sb(name, shape, dt=F):
            return ctx.enter_context(nc.sbuf_tensor(name, shape, dt))

        def ps(name, shape):
            return ctx.enter_context(nc.psum_tensor(name, shape, F))

        def sem(name):
            return ctx.enter_context(nc.semaphore(name))

        wa_hi, wa_lo = sb("wa_hi", [P, KC, L], FR), sb("wa_lo", [P, KC, L], FR)
        wb_hi, wb_lo = sb("wb_hi", [P, KC, L], FR), sb("wb_lo", [P, KC, L], FR)
        wr = sb("wr", [P, KC, 2, CAT], FR)
        lb_hi, lb_lo = sb("lb_hi", [P, L], FR), sb("lb_lo", [P, L], FR)
        bias = sb("bias", [P, KC * CAT])
        bias_r = sb("bias_r", [P, E])
        kst = sb("kst", [P, K_ALL])
        lam_sb = sb("lam_sb", [P, 2])
        dec, turn = sb("dec", [P, H]), sb("turn", [P, H])
        qr, qi = sb("qr", [P, H]), sb("qi", [P, H])
        mul = sb("mul", [P, NM])
        gt, neg_gt, flip = sb("gt", [P, 1]), sb("neg_gt", [P, 1]), sb("flip", [P, 1])
        xn = sb("xn", [P, N, 2])
        xd = sb("xd", [P, 2, 2, N])
        u_t, er_t = sb("u_t", [P, HT, NM]), sb("er_t", [P, HT, NM])
        gh_t = sb("gh_t", [P, 2, HT, NA + NB0])
        g_t, h_t = gh_t[:, 0], gh_t[:, 1]
        k_t = gh_t[:, :, :, :].rearrange("p i h m -> p (i h m)")[:, 0:HT * NM].rearrange("p (h m) -> p h m", h=HT)
        a_t = sb("a_t", [P, HT, NB1])
        xy, pp, qq = sb("xy", [P, 2, HT, NA]), sb("pp", [P, 2, HT, NB1]), sb("qq", [P, 2, HT, NB0])
        t1, t2 = sb("t1", [P, 2, HT, NA]), sb("t2", [P, 2, HT, NA])
        u12 = sb("u12", [P, 2, HT, NA])
        v_sb = sb("v_sb", [P, HT, NA, C])
        b_sb = sb("b_sb", [P, HT, NB1, NB0])
        tmp = sb("tmp", [P, L])
        x1_hi, x1_lo = sb("x1_hi", [P, KC, P], FR), sb("x1_lo", [P, KC, P], FR)
        x2_hi, x2_lo = sb("x2_hi", [P, KC, P], FR), sb("x2_lo", [P, KC, P], FR)
        h1 = sb("h1", [P, L])
        h2 = [sb(f"h2_{i}", [P, L]) for i in range(2)]
        junk = sb("junk", [P, L], BF)
        hw_sb = sb("hw_sb", [P, E, R])
        hw_hi, hw_lo = sb("hw_hi", [P, P], FR), sb("hw_lo", [P, P], FR)
        st1, st2 = sb("st1", [P, 8]), sb("st2", [P, 2, 8])
        gate = sb("gate", [P, 2, E, E])
        gs, tau = sb("gs", [P, 6, E]), sb("tau", [P, 1])
        cat = sb("cat", [P, CAT])
        wb_sum, wb_neg = sb("wb_sum", [P, NWT]), sb("wb_neg", [P, NWT])
        rsum, neg_mean, msum = sb("rsum", [P, 2]), sb("neg_mean", [P, 2]), sb("msum", [P, 2, L // 32])

        acc_a = ps("acc_a", [P, L])
        acc_b = ps("acc_b", [P, L])
        turnp = ps("turnp", [P, L])
        small = ps("small", [P, HALF])
        xps = ps("xps", [P, HALF])

        consts_in, params_in, bias_in, lora_in, lorb_in, rt_in, x_in = (sem(n) for n in (
            "consts_in", "params_in", "bias_in", "lora_in", "lorb_in", "rt_in", "x_in"))
        w_in = [sem(f"w_in{i}") for i in range(2)]
        wb_in = [sem(f"wb_in{i}") for i in range(3)]
        mask_in = [sem("mask_in0"), sem("mask_in1")]
        out_stored = [sem("out_stored0"), sem("out_stored1")]
        pstep, halfstep = sem("pstep"), sem("halfstep")
        mask_summed, blk_ready = sem("mask_summed"), sem("blk_ready")
        w_sum, w_mean, w_centred, w_t, w_hi_ready, w_lo = (sem(n) for n in (
            "w_sum", "w_mean", "w_centred", "w_t", "w_hi_ready", "w_lo"))
        rt_t, rt_copied, cat_mean, cat_centred, cat_hi, cat_lo = (sem(n) for n in (
            "rt_t", "rt_copied", "cat_mean", "cat_centred", "cat_hi", "cat_lo"))
        lorb_hi, lorb_lo = sem("lorb_hi"), sem("lorb_lo")
        x_twice, w_ready, tab_chain, tab_exponent, tab_phase, tab_exp, tab_sin = (sem(n) for n in (
            "x_twice", "w_ready", "tab_chain", "tab_exponent", "tab_phase", "tab_exp", "tab_sin"))
        v_chain, b_chain, v_ready, b_ready = sem("v_chain"), sem("b_chain"), sem("v_ready"), sem("b_ready")
        kt_ready, kt_hi, kt_copied, kt_lo, h1_ready, h1_copied, h1_stat, h1_dev = (sem(n) for n in (
            "kt_ready", "kt_hi", "kt_copied", "kt_lo", "h1_ready", "h1_copied", "h1_stat", "h1_dev"))
        attn_ready, rs1_chain, h2_ready, h2_stat, h2_dev, rs2_chain = (sem(n) for n in (
            "attn_ready", "rs1_chain", "h2_ready", "h2_stat", "h2_dev", "rs2_chain"))
        h2t_ready, h2t_hi, h2t_lo, cat_ready, gate_chain, hw_ready = (sem(n) for n in (
            "h2t_ready", "h2t_hi", "h2t_lo", "cat_ready", "gate_chain", "hw_ready"))
        hwt_ready, hwt_hi, hwt_lo, ffn_ready, bias_added, out_ready = (sem(n) for n in (
            "hwt_ready", "hwt_hi", "hwt_lo", "ffn_ready", "bias_added", "out_ready"))

        ident = kst[:, K_ID:K_ID + P]

        def col(i):
            return kst[:, K_COL + i:K_COL + i + 1]

        flat = lambda b: b[:, :, :, :].rearrange("p x y z -> p (x y z)")
        wa_stage = h2
        wb_stage = [bias[:, 0:L], h2[0][:, :], h2[1][:, :]]
        m_stage = [h1[:, :].bitcast(I32), flat(v_sb).bitcast(I32)]
        rt_rows = E * KC
        rt_stage = hw_sb[0:rt_rows, :, :].rearrange("p e r -> p (e r)")
        lb_stage = h2[1]
        cat_stage = bias[:, :].rearrange("p (k n) -> p k n", k=KC)
        wa_ps, wb_ps = [acc_a, acc_b], [turnp, acc_b]
        blk_ps = [small, xps]
        slot = [b[:, 2 * H * i:2 * H * (i + 1)] for b in (flat(b_sb), tmp) for i in range(4)]
        kt_full = flat(b_sb).rearrange("p (k n) -> p k n", k=KC)

        x_v = x.rearrange("c (t h) n r -> t h c (n r)", h=HT)
        out_v = out.rearrange("c (t h) l -> t h c l", h=HT)
        lora_v = lora_a.rearrange("e (k p) r -> k p e r", p=P)

        LOOP = range(3, TILES - 3)
        FRONT, BACK = range(0, LOOP.start), range(LOOP.stop, TILES + 1)

        def steps(eng, step):
            for t in FRONT:
                step(t, t % 2)
            with eng.Fori(0, len(LOOP) // 2) as i:
                for u in range(2):
                    step(i * 2 + (LOOP.start + u), (LOOP.start + u) % 2)
            for t in BACK:
                step(t, t % 2)

        def wa_tiles(eng, pair_body):
            pair_body(0)
            with eng.Fori(1, NWT // 2) as i:
                pair_body(i * 2)

        def real(t):
            return not isinstance(t, int) or 0 <= t < TILES

        def later(t, first):
            return not isinstance(t, int) or t >= first

        def at(t, n):
            return isinstance(t, int) and t == n

        block = ctx.enter_context(nc.Block())

        @block.sync
        def _(sp):
            def load_x(t):
                if later(t, 1):
                    sp.wait_ge(x_twice, t)
                sp.dma_start(xn[:, :, :].rearrange("p n r -> p (n r)"), x_v[t]).then_inc(x_in, 16)

            sp.dma_start(slot[4], log_dt.rearrange("h r -> (h r)").partition_broadcast(P)).then_inc(params_in, 16)
            sp.dma_start(lam_sb[0:N, :], lam).then_inc(params_in, 16)
            sp.dma_start(lam_sb[N:P, :], lam).then_inc(params_in, 16)
            sp.dma_start(kst[:, :], consts).then_inc(consts_in, 16)

            def load_wa(j0):
                for u in range(2):
                    j = j0 + u
                    if later(j, 2):
                        sp.wait_ge(mask_summed, j - 1)
                    sp.dma_start(m_stage[u], mask[bass.ds(j * P, P), :]).then_inc(mask_in[u], 16)
                    if later(j, 2):
                        sp.wait_ge(w_t, j - 1)
                    sp.dma_start(wa_stage[u][:, :], w_attn[bass.ds(j * P, P), :]).then_inc(w_in[u], 16)
                if not later(j0, 2):
                    load_x(0)
                    sp.dma_start(wb_stage[0], w_base[0:P, :]).then_inc(wb_in[0], 16)
                    sp.dma_start(rt_stage, w_router.rearrange("e (k p) -> (e k) p", p=P)).then_inc(rt_in, 16)

            wa_tiles(sp, load_wa)
            for j in range(1, NWT):
                sp.wait_ge(w_t, NWT - 2 + j if j < 3 else NWT + j - 2)
                sp.dma_start(wb_stage[j % 3], w_base[j * P:(j + 1) * P, :]).then_inc(wb_in[j % 3], 16)
                if j == 2:
                    load_x(1)
            sp.wait_ge(w_t, 2 * NWT - 1)
            for k in range(KC):
                sp.dma_start(cat_stage[:, k, 0:E * R].rearrange("p (e r) -> p e r", e=E), lora_v[k]).then_inc(lora_in, 16)
            sp.dma_start(lb_stage[:, :], lora_b.rearrange("e r l -> (e r) l")).then_inc(lorb_in, 16)
            load_x(2)
            sp.wait_ge(cat_lo, 1)
            sp.dma_start(bias[:, 0:L], b_base.partition_broadcast(P)).then_inc(bias_in, 16)
            sp.dma_start(bias_r[:, :], b_router.partition_broadcast(P)).then_inc(bias_in, 16)

            def step(t, par):
                if real(t + 3):
                    load_x(t + 3)
                if real(t - 1):
                    sp.wait_ge(out_ready, t)
                    sp.dma_start(out_v[t - 1], h2[1 - par][:, :]).then_inc(out_stored[1 - par], 16)

            steps(sp, step)
            sp.wait_ge(out_stored[0], 8 * TILES)
            sp.wait_ge(out_stored[1], 8 * TILES)

        @block.tensor
        def _(pe):
            def block_sums(j, u):
                pe.wait_ge(mask_summed, j + 1)
                if later(j, 2):
                    pe.wait_ge(w_sum, j - 1)
                pe.matmul(blk_ps[u][:, 0:L // 32], kst[:, K_BLK:K_BLK + P], msum[:, u, :],
                          start=True, stop=True).then_inc(blk_ready, 1)

            def weight_transposes(j, banks, stage):
                pe.wait_ge(w_centred, j + 1)
                if later(j, 2):
                    pe.wait_ge(w_lo, j - 1)
                for k in range(KC):
                    mm = pe.transpose(banks[:, k * P:(k + 1) * P], stage[:, k * P:(k + 1) * P], ident)
                mm.then_inc(w_t, 1)

            def wa_pair(j):
                for u in range(2):
                    block_sums(j + u, u)
                for u in range(2):
                    weight_transposes(j + u, wa_ps[u], wa_stage[u])

            def x_transposes(t):
                pe.wait_ge(x_twice, t + 1)
                if later(t, 1):
                    pe.wait_ge(v_ready, t)
                for r in range(2):
                    mm = pe.transpose(xps[:, r * P:(r + 1) * P], xd[:, r, :, :].rearrange("p d n -> p (d n)"), ident)
                mm.then_inc(w_ready, 1)

            def k_transposed(t):
                pe.wait_ge(v_ready, t + 1)
                pe.wait_ge(b_ready, t + 1)
                for h in range(HT):
                    mm = pe.matmul(turnp[:, h * P:(h + 1) * P], b_sb[:, h, :, :].rearrange("p x y -> p (x y)"),
                                   v_sb[:, h, :, :].rearrange("p a c -> p (a c)"), start=True, stop=True)
                mm.then_inc(kt_ready, 1)

            def k_rows(t):
                pe.wait_ge(kt_hi, t + 1)
                pe.wait_ge(kt_copied, t + 1)
                for k in range(KC):
                    mm = pe.transpose(turnp[:, k * P:(k + 1) * P], kt_full[:, k, :], ident)
                mm.then_inc(h1_ready, 1)

            def h2_transposes(t, par):
                pe.wait_ge(h2_ready, t + 1)
                for k in range(KC):
                    mm = pe.transpose(turnp[:, k * P:(k + 1) * P], h2[par][:, k * P:(k + 1) * P], ident)
                mm.then_inc(h2t_ready, 1)

            def product(acc, hi, lo, w_hi, w_lo, first, last):
                for a, w, n in ((hi, w_hi, 0), (hi, w_hi, 1), (hi, w_lo, 0), (hi, w_lo, 1), (lo, w_hi, 0), (lo, w_hi, 1)):
                    cols = slice(n * HALF, (n + 1) * HALF)
                    mm = pe.matmul(acc[:, cols], a, w[:, cols], start=first and a is hi and w is w_hi,
                                   stop=last and a is lo)
                return mm

            def step(t, par):
                if real(t - 1):
                    if at(t, 1):
                        pe.wait_ge(w_lo, 2 * NWT)
                    if real(t):
                        pe.wait_ge(h1_copied, t + 1)
                        h2_transposes(t - 1, 1 - par)
                if real(t):
                    pe.wait_ge(kt_lo, t + 1)
                    for k in range(KC):
                        mm = product(acc_a, x1_hi[:, k, :], x1_lo[:, k, :], wa_hi[:, k, :], wa_lo[:, k, :],
                                     k == 0, k == KC - 1)
                        if k == KC - 1:
                            mm.then_inc(attn_ready, 1)
                        if at(t, 0):
                            weight_transposes(NWT + k, wb_ps[k % 2], wb_stage[k % 3])
                if real(t - 1):
                    pe.wait_ge(h2t_lo, t)
                if at(t, 0):
                    pe.wait_ge(w_lo, 2 * NWT)
                if real(t + 1):
                    k_transposed(t + 1)
                if at(t, 0):
                    pe.wait_ge(rt_copied, 1)
                    pe.wait_ge(lora_in, 16 * KC)
                    for k in range(KC):
                        mm = pe.matmul(small[:, 0:CAT], kst[:, K_MEAN:K_MEAN + P], cat_stage[:, k, :],
                                       start=k == 0, stop=k == KC - 1)
                    mm.then_inc(cat_mean, 1)
                if real(t - 1):
                    if at(t, 1):
                        pe.wait_ge(cat_lo, 1)
                    if later(t, 2):
                        pe.wait_ge(hwt_lo, t - 1)
                    for k in range(KC):
                        pe.matmul(small[:, 0:2 * CAT], x2_hi[:, k, :], wr[:, k, :, :].rearrange("p s n -> p (s n)"),
                                  start=k == 0, stop=False)
                        mm = pe.matmul(small[:, 0:CAT], x2_lo[:, k, :], wr[:, k, 0, :], start=False, stop=k == KC - 1)
                    mm.then_inc(cat_ready, 1)
                    if later(t, 2):
                        pe.wait_ge(out_ready, t - 1)
                for k in range(KC):
                    if k == 2 and real(t + 2):
                        x_transposes(t + 2)
                    if k == KC // 2 and real(t + 1):
                        k_rows(t + 1)
                    if k == KC // 2 and at(t, TILES - 1):
                        h2_transposes(t, par)
                    if k == KC - 2 and real(t - 1):
                        pe.wait_ge(hw_ready, t)
                        pe.transpose(small[:, 0:P], hw_sb[:, :, :].rearrange("p e r -> p (e r)"), ident)\
                            .then_inc(hwt_ready, 1)
                    if real(t - 1):
                        product(acc_b, x2_hi[:, k, :], x2_lo[:, k, :], wb_hi[:, k, :], wb_lo[:, k, :], k == 0, False)
                if real(t - 1):
                    if at(t, 1):
                        pe.wait_ge(lorb_lo, 1)
                    pe.wait_ge(hwt_lo, t)
                    product(acc_b, hw_hi[:, :], hw_lo[:, :], lb_hi[:, :], lb_lo[:, :], False, True)\
                        .then_inc(ffn_ready, 1)

            pe.wait_ge(consts_in, 16)
            wa_tiles(pe, wa_pair)
            pe.wait_ge(w_lo, NWT)
            x_transposes(0)
            k_transposed(0)
            x_transposes(1)
            pe.wait_ge(rt_in, 16)
            pe.transpose(small[:, 0:rt_rows], rt_stage, ident[0:rt_rows, 0:rt_rows]).then_inc(rt_t, 1)
            k_rows(0)
            pe.wait_ge(h1_copied, 1)
            steps(pe, step)

        @block.scalar
        def _(act):
            def wa_pair(j0):
                for u in range(2):
                    j = j0 + u
                    act.wait_ge(w_sum, j + 1)
                    act.activation(neg_mean[:, u:u + 1], rsum[:, u:u + 1], ACT.Copy, scale=-1.0 / L).then_inc(w_mean, 1)
                    act.wait_ge(w_mean, j + 1)
                    act.activation(wa_stage[u][:, :], wa_stage[u][:, :], ACT.Identity, bias=neg_mean[:, u:u + 1])\
                        .then_inc(w_centred, 1)
                for u in range(2):
                    j = j0 + u
                    act.wait_ge(w_t, j + 1)
                    act.activation(wa_hi[:, :, bass.ds(j * P, P)], wa_ps[u][:, :].rearrange("p (k n) -> p k n", k=KC),
                                   ACT.Copy).then_inc(w_hi_ready, 1)

            def wb_mean(j):
                act.wait_ge(wb_in[j % 3], 16 * (j // 3 + 1))
                act.activation(junk[:, :], wb_stage[j % 3], ACT.Copy, accum_out=wb_sum[:, j:j + 1]).then_inc(w_sum, 1)
                act.wait_ge(w_sum, NWT + j + 1)
                act.activation(wb_neg[:, j:j + 1], wb_sum[:, j:j + 1], ACT.Copy, scale=-1.0 / L).then_inc(w_mean, 1)

            def wb_high(j):
                act.wait_ge(w_t, NWT + j + 1)
                act.activation(wb_hi[:, :, j * P:(j + 1) * P], wb_ps[j % 2][:, :].rearrange("p (k n) -> p k n", k=KC),
                               ACT.Copy).then_inc(w_hi_ready, 1)

            def x_rows_twice(t):
                act.wait_ge(x_in, t * 16 + 16)
                if later(t, 1):
                    act.wait_ge(w_ready, t)
                for r in range(2):
                    op = act.activation(xd[:, r, :, :], xn[:, :, r].unsqueeze(1).to_broadcast([P, 2, N]), ACT.Copy)
                op.then_inc(x_twice, 1)

            def exp_and_sin(t):
                act.wait_ge(tab_exponent, t + 1)
                act.activation(er_t[:, :, :], er_t[:, :, :], ACT.Exp).then_inc(tab_exp, 1)
                act.wait_ge(tab_phase, t + 1)
                g_a, g_b0 = g_t[:, :, 0:NA], g_t[:, :, NA:NA + NB0]
                h_a, h_b0 = h_t[:, :, 0:NA], h_t[:, :, NA:NA + NB0]
                act.activation(xy[:, 0], g_a, ACT.Sin, scale=-TWO_PI, bias=col(COL_BX))
                act.activation(xy[:, 1], h_a, ACT.Sin, scale=col(COL_S), bias=col(COL_BY))
                act.activation(pp[:, 0], a_t[:, :, :], ACT.Sin, scale=-TWO_PI, bias=col(COL_HALF))
                act.activation(pp[:, 1], u_t[:, :, SB1], ACT.Sin, scale=col(COL_S))
                act.activation(qq[:, 0], g_b0, ACT.Sin, scale=col(COL_S), bias=col(COL_BX))
                act.activation(qq[:, 1], h_b0, ACT.Sin, scale=col(COL_NS), bias=col(COL_BQ))\
                    .then_inc(tab_sin, 1)

            def k_high(t):
                by_head = turnp[:, :].rearrange("p (h a c) -> p h a c", h=HT, a=NA)
                act.wait_ge(kt_ready, t + 1)
                act.activation(kt_full.rearrange("p a (h c) -> p h a c", c=C), by_head, ACT.Copy).then_inc(kt_copied, 1)
                if later(t, 1):
                    act.wait_ge(attn_ready, t)
                act.activation(x1_hi[:, :, :].rearrange("p a (h c) -> p h a c", c=C), by_head, ACT.Copy)\
                    .then_inc(kt_hi, 1)

            def deviation(s, src, stat, dev, t):
                act.activation(s[:, 1:2], s[:, 0:1], ACT.Copy, scale=-1.0 / L).then_inc(stat, 1)
                act.wait_ge(stat, t * 2 + 1)
                act.activation(junk[:, :], src, ACT.Square, bias=s[:, 1:2], accum_out=s[:, 2:3]).then_inc(stat, 1)
                act.wait_ge(stat, t * 2 + 2)
                act.activation(s[:, 3:4], s[:, 2:3], ACT.Sqrt, scale=1.0 / L, bias=col(COL_EPS)).then_inc(dev, 1)

            def k_copy(t):
                act.wait_ge(h1_ready, t + 1)
                if later(t, 1):
                    act.wait_ge(h2_ready, t)
                act.activation(h1[:, :], turnp[:, :], ACT.Copy, accum_out=st1[:, 0:1]).then_inc(h1_copied, 1)
                act.wait_ge(h1_copied, t + 1)
                deviation(st1, h1[:, :], h1_stat, h1_dev, t)

            def step(t, par):
                if real(t - 1):
                    act.wait_ge(h2t_ready, t)
                    if later(t, 2):
                        act.wait_ge(ffn_ready, t - 1)
                    act.activation(x2_hi[:, :, :].rearrange("p k n -> p (k n)"), turnp[:, :], ACT.Copy).then_inc(h2t_hi, 1)
                if at(t, 0):
                    for j in range(NWT):
                        wb_high(j)
                        if j + 3 < NWT:
                            wb_mean(j + 3)
                if real(t + 2):
                    exp_and_sin(t + 2)
                    x_rows_twice(t + 2)
                if real(t + 1):
                    k_high(t + 1)
                if real(t):
                    act.wait_ge(h2_ready, t + 1)
                    deviation(st2[:, par, :], h2[par][:, :], h2_stat, h2_dev, t)
                if real(t + 1):
                    k_copy(t + 1)
                if at(t, 0):
                    act.wait_ge(cat_centred, 1)
                    act.activation(wr[:, :, 0, :], cat_stage, ACT.Copy).then_inc(cat_hi, 1)
                    act.wait_ge(lorb_in, 16)
                    act.activation(lb_hi[:, :], lb_stage[:, :], ACT.Copy).then_inc(lorb_hi, 1)
                if real(t - 1):
                    act.wait_ge(hwt_ready, t)
                    act.activation(hw_hi[:, :], small[:, 0:P], ACT.Copy).then_inc(hwt_hi, 1)

            act.wait_ge(consts_in, 16)
            act.wait_ge(pstep, P_ARGS)
            act.activation(slot[5], slot[1], ACT.Tanh, scale=0.5)
            act.activation(slot[6], slot[2], ACT.Sin, scale=TWO_PI)
            act.activation(slot[7], slot[2], ACT.Sin, scale=TWO_PI / 2).then_inc(halfstep, 1)
            wa_tiles(act, wa_pair)
            x_rows_twice(0)
            exp_and_sin(0)
            for j in range(3):
                wb_mean(j)
            x_rows_twice(1)
            k_high(0)
            k_copy(0)
            exp_and_sin(1)
            steps(act, step)

        @block.gpsimd
        def _(pool):
            for j in range(NWT):
                pool.wait_ge(w_mean, NWT + j + 1)
                w = wb_stage[j % 3]
                pool.tensor_scalar(w, w, 1.0, wb_neg[:, j:j + 1], ALU.mult, ALU.add).then_inc(w_centred, 1)

            def step(t, par):
                if real(t - 1):
                    pool.wait_ge(h2t_ready, t)
                    pool.wait_ge(h2_dev, t)
                    h = h2[1 - par][:, :]
                    pool.tensor_tensor(h, h, bias[:, 0:L], ALU.add).then_inc(bias_added, 1)

            pool.wait_ge(bias_in, 32)
            steps(pool, step)

        @block.vector
        def _(dve):
            def chained(s, base):
                n = [base]

                def link(op):
                    op.then_inc(s, 1)
                    n[0] = n[0] + 1
                    dve.wait_ge(s, n[0])
                return link

            def dve_arguments():
                link = chained(pstep, 0)
                x_, k_, r_, p_, w_ = slot[4], slot[0], slot[1], slot[2], slot[3]
                link(dve.tensor_scalar(k_, x_, LOG2E, ROUND, ALU.mult, ALU.add))
                link(dve.tensor_scalar(k_, k_, ROUND, None, ALU.subtract))
                link(dve.tensor_scalar(k_, k_, -126.0, 127.0, ALU.max, ALU.min))
                link(dve.scalar_tensor_tensor(r_, k_, -LN2_HI, x_, ALU.mult, ALU.add))
                link(dve.scalar_tensor_tensor(r_, k_, -LN2_LO, r_, ALU.mult, ALU.add))
                link(dve.tensor_scalar(w_.bitcast(I32), k_, 127.0, 8388608.0, ALU.add, ALU.mult))
                link(dve.tensor_scalar(p_, r_, 1.0 / 5040, None, ALU.mult))
                for c in (1.0 / 720, 1.0 / 120, 1.0 / 24, 1.0 / 6, 0.5, 1.0):
                    link(dve.scalar_tensor_tensor(p_, p_, c, r_, ALU.add, ALU.mult))
                link(dve.scalar_tensor_tensor(p_, p_, 1.0, w_, ALU.add, ALU.mult))
                dt = p_.rearrange("p (h r) -> p r h", r=2)
                lr, li = lam_sb[:, 0:1], lam_sb[:, 1:2]
                dve.tensor_scalar(dec[:, :], dt[:, 0, :], lr, None, ALU.mult)
                dve.tensor_scalar(gt[:, :], lr, 0.0, None, ALU.is_gt)
                link(dve.tensor_scalar(turn[:, :], dt[:, 1, :], li, None, ALU.mult))
                dve.tensor_scalar(neg_gt[:, :], gt[:, :], -1.0, None, ALU.mult)
                dve.tensor_scalar(flip[:, :], gt[:, :], -2.0, 1.0, ALU.mult, ALU.add)
                link(dve.tensor_scalar(turn[:, :], turn[:, :], INV_TWO_PI, None, ALU.mult))
                dve.scalar_tensor_tensor(mul[:, :], kst[:, K_OFF:K_OFF + NM], neg_gt[:, 0:1], kst[:, K_MUL:K_MUL + NM],
                                         ALU.mult, ALU.add)
                two = lambda s: s.rearrange("p (s h) -> p s h", s=2)
                a_, f_ = slot[1], slot[2]
                dve.tensor_scalar(two(a_)[:, 0], dec[:, :], flip[:, 0:1], None, ALU.mult)
                link(dve.tensor_scalar(two(f_)[:, 0], turn[:, :], flip[:, 0:1], None, ALU.mult))
                dve.tensor_scalar(two(a_)[:, 1], two(a_)[:, 0], float(L), None, ALU.mult)
                link(dve.tensor_scalar(two(f_)[:, 1], two(f_)[:, 0], float(L), None, ALU.mult))
                link(dve.tensor_scalar(slot[3], f_, ROUND, -ROUND, ALU.add, ALU.add))
                link(dve.tensor_tensor(f_, f_, slot[3], ALU.subtract))

            def dve_parameters():
                link = chained(pstep, P_ARGS)
                two = lambda s: s.rearrange("p (s h) -> p s h", s=2)
                lr, li = lam_sb[:, 0:1], lam_sb[:, 1:2]
                dve.wait_ge(halfstep, 1)
                th, s_, sh = slot[5], slot[6], slot[7]
                link(dve.tensor_scalar(slot[0], th, -1.0, 1.0, ALU.mult, ALU.add))
                link(dve.reciprocal(slot[3], slot[0]))
                link(dve.scalar_tensor_tensor(th, th, 2.0, slot[3], ALU.mult, ALU.mult))
                link(dve.scalar_tensor_tensor(sh, sh, 2.0, sh, ALU.mult, ALU.mult))
                link(dve.tensor_scalar(slot[0], sh, -1.0, 1.0, ALU.mult, ALU.add))
                link(dve.tensor_tensor(slot[3], th, slot[0], ALU.mult))
                link(dve.tensor_tensor(slot[3], slot[3], sh, ALU.subtract))
                link(dve.scalar_tensor_tensor(s_, th, 1.0, s_, ALU.add, ALU.mult))
                nr, dr, ni, di = two(slot[3])[:, 0], two(slot[3])[:, 1], two(s_)[:, 0], two(s_)[:, 1]
                d_r, d_i = two(slot[4])[:, 0], two(slot[4])[:, 1]
                w0, w1 = two(slot[0])[:, 0], two(slot[0])[:, 1]
                dve.tensor_scalar(w0, di, li, None, ALU.mult)
                link(dve.tensor_scalar(w1, di, lr, None, ALU.mult))
                dve.scalar_tensor_tensor(d_r, dr, lr, w0, ALU.mult, ALU.subtract)
                link(dve.scalar_tensor_tensor(d_i, dr, li, w1, ALU.mult, ALU.add))
                m0, m1 = two(slot[1])[:, 0], two(slot[1])[:, 1]
                dve.tensor_tensor(m0, d_r, d_r, ALU.mult)
                link(dve.tensor_tensor(m1, d_i, d_i, ALU.mult))
                link(dve.tensor_tensor(m0, m0, m1, ALU.add))
                link(dve.tensor_scalar(m0, m0, REC_EPS, None, ALU.add))
                link(dve.reciprocal(m1, m0))
                a0, a1 = two(slot[2])[:, 0], two(slot[2])[:, 1]
                b0, b1 = two(slot[5])[:, 0], two(slot[5])[:, 1]
                dve.tensor_tensor(a0, nr, d_r, ALU.mult)
                dve.tensor_tensor(a1, ni, d_i, ALU.mult)
                dve.tensor_tensor(b0, ni, d_r, ALU.mult)
                link(dve.tensor_tensor(b1, nr, d_i, ALU.mult))
                dve.tensor_tensor(a0, a0, a1, ALU.add)
                link(dve.tensor_tensor(b0, b0, b1, ALU.subtract))
                dve.tensor_tensor(qr[:, :], a0, m1, ALU.mult)
                link(dve.tensor_tensor(qi[:, :], b0, m1, ALU.mult))

            def wa_sums(j0):
                for u in range(2):
                    dve.wait_ge(mask_in[u], j0 * 8 + 16)
                    dve.tensor_reduce(msum[:, u, :], m_stage[u].rearrange("p (k b) -> p k b", b=32), AX.X, ALU.add)\
                        .then_inc(mask_summed, 1)

            def wa_masked(j0):
                for u in range(2):
                    j = j0 + u
                    dve.wait_ge(blk_ready, j + 1)
                    dve.wait_ge(w_in[u], j0 * 8 + 16)
                    if later(j, 2):
                        dve.wait_ge(w_mean, j - 1)
                    w3 = wa_stage[u][:, :].rearrange("p (k b) -> p k b", b=32)
                    dve.scalar_tensor_tensor(w3, blk_ps[u][:, 0:L // 32].unsqueeze(2).to_broadcast([P, L // 32, 32]), 0.0,
                                             w3, ALU.is_gt, ALU.mult, accum_out=rsum[:, u:u + 1]).then_inc(w_sum, 1)

            def wa_low(j0):
                for u in range(2):
                    j = j0 + u
                    dve.wait_ge(w_hi_ready, j + 1)
                    cols = bass.ds(j * P, P)
                    dve.tensor_tensor(wa_lo[:, :, cols], wa_ps[u][:, :].rearrange("p (k n) -> p k n", k=KC),
                                      wa_hi[:, :, cols].bitcast(F), ALU.subtract).then_inc(w_lo, 1)

            def wb_low(j):
                dve.wait_ge(w_hi_ready, NWT + j + 1)
                cols = slice(j * P, (j + 1) * P)
                dve.tensor_tensor(wb_lo[:, :, cols], wb_ps[j % 2][:, :].rearrange("p (k n) -> p k n", k=KC),
                                  wb_hi[:, :, cols].bitcast(F), ALU.subtract).then_inc(w_lo, 1)

            def over_j(v, n):
                return v.unsqueeze(2).to_broadcast([P, HT, n])

            def decay(s, n):
                return er_t[:, :, s].unsqueeze(1).to_broadcast([P, 2, HT, n])

            def whole(b):
                return b[:, :, :, :]

            def phases(t):
                link = chained(tab_chain, t * 3)
                heads = bass.ds(t * HT, HT)
                m = mul[:, :].unsqueeze(1).to_broadcast([P, HT, NM])
                dve.tensor_tensor(er_t[:, :, :], over_j(dec[:, heads], NM), m, ALU.mult).then_inc(tab_exponent, 1)
                link(dve.tensor_tensor(u_t[:, :, :], over_j(turn[:, heads], NM), m, ALU.mult))
                link(dve.tensor_scalar(k_t, u_t[:, :, :], ROUND, -ROUND, ALU.add, ALU.add))
                link(dve.tensor_tensor(u_t[:, :, :], u_t[:, :, :], k_t, ALU.subtract))
                ab = u_t[:, :, 0:NA + NB0]
                dve.scalar_tensor_tensor(g_t, ab, col(COL_G), ab, ALU.mult, ALU.max)
                dve.scalar_tensor_tensor(h_t, ab, col(COL_H), ab, ALU.mult, ALU.max)
                dve.scalar_tensor_tensor(a_t[:, :, :], u_t[:, :, SB1], -1.0, u_t[:, :, SB1], ALU.mult, ALU.max)\
                    .then_inc(tab_phase, 1)

            def table_v(t):
                heads = bass.ds(t * HT, HT)

                def q(v):
                    return v[:, heads].unsqueeze(1).unsqueeze(3).to_broadcast([P, 2, HT, NA])

                def w(r):
                    rows = xps[:, r * P:(r + 1) * P].rearrange("p (h c) -> p h c", c=C)
                    return rows.unsqueeze(2).to_broadcast([P, HT, NA, C])

                def u(i):
                    return u12[:, i].unsqueeze(3).to_broadcast([P, HT, NA, C])

                tmp4 = tmp[:, :].rearrange("p (h a c) -> p h a c", h=HT, a=NA)
                dve.wait_ge(tab_sin, t + 1)
                dve.tensor_tensor(whole(xy), whole(xy), decay(SA, NA), ALU.mult).then_inc(v_chain, 1)
                dve.wait_ge(v_chain, t * 4 + 1)
                dve.tensor_tensor(whole(t1), whole(xy), q(qr), ALU.mult)
                dve.tensor_tensor(whole(t2), whole(xy), q(qi), ALU.mult).then_inc(v_chain, 1)
                dve.wait_ge(v_chain, t * 4 + 2)
                dve.tensor_tensor(u12[:, 0], t1[:, 0], t2[:, 1], ALU.add)
                dve.tensor_tensor(u12[:, 1], t1[:, 1], t2[:, 0], ALU.subtract).then_inc(v_chain, 1)
                dve.wait_ge(w_ready, t + 1)
                if later(t, 1):
                    dve.wait_ge(kt_ready, t)
                    dve.wait_ge(b_ready, t)
                dve.wait_ge(v_chain, t * 4 + 3)
                dve.tensor_tensor(whole(v_sb), w(0), u(0), ALU.mult)
                dve.tensor_tensor(tmp4, w(1), u(1), ALU.mult).then_inc(v_chain, 1)
                dve.wait_ge(v_chain, t * 4 + 4)
                dve.tensor_tensor(whole(v_sb), whole(v_sb), tmp4, ALU.add).then_inc(v_ready, 1)

            def table_b(t):
                def factors(i):
                    return (pp[:, i].unsqueeze(3).to_broadcast([P, HT, NB1, NB0]),
                            qq[:, i].unsqueeze(2).to_broadcast([P, HT, NB1, NB0]))

                tmpb = tmp[:, :].rearrange("p (h x y) -> p h x y", h=HT, x=NB1)
                dve.wait_ge(tab_sin, t + 1)
                dve.tensor_tensor(whole(pp), whole(pp), decay(SB1, NB1), ALU.mult)
                dve.tensor_tensor(whole(qq), whole(qq), decay(SB0, NB0), ALU.mult).then_inc(b_chain, 1)
                if later(t, 1):
                    dve.wait_ge(h1_ready, t)
                    dve.wait_ge(kt_lo, t)
                dve.wait_ge(v_ready, t + 1)
                dve.wait_ge(b_chain, t * 2 + 1)
                dve.tensor_tensor(whole(b_sb), *factors(0), ALU.mult)
                dve.tensor_tensor(tmpb, *factors(1), ALU.mult).then_inc(b_chain, 1)
                dve.wait_ge(b_chain, t * 2 + 2)
                dve.tensor_tensor(whole(b_sb), whole(b_sb), tmpb, ALU.add).then_inc(b_ready, 1)

            def k_low(t):
                dve.wait_ge(kt_copied, t + 1)
                dve.wait_ge(kt_hi, t + 1)
                dve.tensor_tensor(x1_lo[:, :, :], kt_full, x1_hi[:, :, :].bitcast(F), ALU.subtract).then_inc(kt_lo, 1)

            def reciprocal_deviation(s, dev, s_chain, t):
                dve.wait_ge(dev, t + 1)
                dve.tensor_scalar(s[:, 4:5], s[:, 2:3], 1.0 / L, LN_EPS, ALU.mult, ALU.add)
                dve.reciprocal(s[:, 5:6], s[:, 3:4]).then_inc(s_chain, 1)
                dve.wait_ge(s_chain, t * 4 + 1)
                dve.scalar_tensor_tensor(s[:, 6:7], s[:, 5:6], s[:, 5:6], s[:, 4:5], ALU.mult, ALU.mult).then_inc(s_chain, 1)
                dve.wait_ge(s_chain, t * 4 + 2)
                dve.tensor_scalar(s[:, 7:8], s[:, 6:7], -0.5, 1.5, ALU.mult, ALU.add).then_inc(s_chain, 1)
                dve.wait_ge(s_chain, t * 4 + 3)
                dve.tensor_tensor(s[:, 4:5], s[:, 5:6], s[:, 7:8], ALU.mult).then_inc(s_chain, 1)

            def gates(t, par):
                link = chained(gate_chain, t * 9)
                z, cnt, tot, inv, cand, w = (gs[:, i, :] for i in range(6))
                z_j = z.unsqueeze(1).to_broadcast([P, E, E])
                z_i = z.unsqueeze(2).to_broadcast([P, E, E])
                dve.wait_ge(cat_ready, t + 1)
                dve.wait_ge(rs2_chain, t * 4 + 4)
                link(dve.tensor_copy(cat[:, :], small[:, CAT:2 * CAT]))
                link(dve.tensor_tensor(cat[:, :], small[:, 0:CAT], cat[:, :], ALU.add))
                link(dve.scalar_tensor_tensor(z, cat[:, E * R:CAT], st2[:, par, 4:5], bias_r[:, :], ALU.mult, ALU.add))
                link(dve.tensor_tensor(gate[:, 0], z_j, z_i, ALU.is_ge))
                dve.tensor_reduce(cnt, gate[:, 0], AX.X, ALU.add)
                link(dve.tensor_tensor(gate[:, 1], gate[:, 0], z_j, ALU.mult))
                dve.reciprocal(inv, cnt)
                link(dve.tensor_reduce(tot, gate[:, 1], AX.X, ALU.add))
                link(dve.scalar_tensor_tensor(cand, tot, -1.0, inv, ALU.add, ALU.mult))
                link(dve.tensor_reduce(tau[:, :], cand, AX.X, ALU.max))
                link(dve.tensor_scalar(w, z, tau[:, 0:1], 0.0, ALU.subtract, ALU.max))
                dve.tensor_tensor(hw_sb[:, :, :], cat[:, 0:E * R].rearrange("p (e r) -> p e r", e=E),
                                  w.unsqueeze(2).to_broadcast([P, E, R]), ALU.mult).then_inc(hw_ready, 1)

            def step(t, par):
                if real(t - 1):
                    reciprocal_deviation(st2[:, 1 - par, :], h2_dev, rs2_chain, t - 1)
                    dve.wait_ge(h2t_hi, t)
                    dve.tensor_tensor(x2_lo[:, :, :].rearrange("p k n -> p (k n)"), turnp[:, :],
                                      x2_hi[:, :, :].bitcast(F).rearrange("p k n -> p (k n)"), ALU.subtract)\
                        .then_inc(h2t_lo, 1)
                if at(t, 0):
                    for j in range(NWT):
                        wb_low(j)
                    dve.wait_ge(rt_t, 1)
                    dve.wait_ge(w_t, 2 * NWT - 1)
                    dve.tensor_copy(cat_stage[:, :, E * R:CAT],
                                    small[:, 0:rt_rows].rearrange("p (e k) -> p k e", e=E)).then_inc(rt_copied, 1)
                if real(t):
                    reciprocal_deviation(st1, h1_dev, rs1_chain, t)
                if real(t + 1):
                    table_b(t + 1)
                if real(t + 2):
                    phases(t + 2)
                if real(t):
                    dve.wait_ge(attn_ready, t + 1)
                    dve.wait_ge(rs1_chain, t * 4 + 4)
                    if later(t, 2):
                        dve.wait_ge(out_stored[par], t * 8 - 8 * par)
                    dve.scalar_tensor_tensor(h2[par][:, :], acc_a[:, :], st1[:, 4:5], h1[:, :], ALU.mult, ALU.add,
                                             accum_out=st2[:, par, 0:1]).then_inc(h2_ready, 1)
                if real(t + 1):
                    k_low(t + 1)
                if at(t, 0):
                    dve.wait_ge(cat_mean, 1)
                    dve.tensor_tensor(cat_stage, cat_stage, small[:, 0:CAT].unsqueeze(1).to_broadcast([P, KC, CAT]),
                                      ALU.subtract).then_inc(cat_centred, 1)
                    dve.wait_ge(cat_hi, 1)
                    dve.tensor_tensor(wr[:, :, 1, :], cat_stage, wr[:, :, 0, :].bitcast(F), ALU.subtract).then_inc(cat_lo, 1)
                    dve.wait_ge(lorb_hi, 1)
                    dve.tensor_tensor(lb_lo[:, :], lb_stage[:, :], lb_hi[:, :].bitcast(F), ALU.subtract).then_inc(lorb_lo, 1)
                if at(t, 1):
                    dve.wait_ge(bias_in, 32)
                if real(t - 1):
                    gates(t - 1, 1 - par)
                if real(t + 2):
                    table_v(t + 2)
                if real(t - 1):
                    dve.wait_ge(hwt_hi, t)
                    dve.tensor_tensor(hw_lo[:, :], small[:, 0:P], hw_hi[:, :].bitcast(F), ALU.subtract).then_inc(hwt_lo, 1)
                    dve.wait_ge(ffn_ready, t)
                    dve.wait_ge(bias_added, t)
                    h = h2[1 - par][:, :]
                    dve.scalar_tensor_tensor(h, acc_b[:, :], st2[:, 1 - par, 4:5], h, ALU.mult, ALU.add).then_inc(out_ready, 1)

            dve.wait_ge(params_in, 48)
            dve.wait_ge(consts_in, 16)
            dve_arguments()
            wa_sums(0)
            dve_parameters()
            wa_masked(0)
            with dve.Fori(1, NWT // 2) as i:
                wa_sums(i * 2)
                wa_masked(i * 2)
                wa_low(i * 2 - 2)
            wa_low(NWT - 2)
            phases(0)
            table_v(0)
            table_b(0)
            phases(1)
            k_low(0)
            table_v(1)
            steps(dve, step)


_INS = ['x', 'L0_tok_log_dt', 'L0_tok_Lambda', 'L0_attn_weight', 'L0_attn_mask', 'L0_ffn_W_base', 'L0_ffn_b_base',
        'L0_ffn_W_router', 'L0_ffn_b_router', 'L0_ffn_lora_A', 'L0_ffn_lora_B']


def kernel(**inputs):
    import numpy as _np
    import concourse.bacc as _bacc
    from concourse import mybir as _mybir
    from concourse.bass_utils import run_bass_kernel_spmd as _run

    nc = _bacc.Bacc("TRN2", target_bir_lowering=False, num_devices=1)
    arrays, args = {}, []
    for name in _INS:
        arrays[f"in_{name}"] = _np.ascontiguousarray(inputs[name])
    arrays["in_consts"] = constants()
    for name, a in arrays.items():
        args.append(nc.dram_tensor(name, a.shape, _mybir.dt.from_np(a.dtype), kind="ExternalInput").ap())
    out = nc.dram_tensor("out", (C, H, L), _mybir.dt.float32, kind="ExternalOutput").ap()
    build_vit_tower(nc, *args, out)
    return _run(nc, [arrays], core_ids=[0]).results[0]["out"]
```

```python
import concourse.bass as bass
from concourse import mybir
from contextlib import ExitStack


C, H, N, L = 16, 128, 64, 1024
E, R = 8, 16
P = 128
HT = P // C
TILES = H // HT
KC = L // P
HALF = 512
NA, NB1, NB0 = 8, 8, 16
NM = NA + NB0 + NB1
SA, SB0, SB1 = slice(0, NA), slice(NA, NA + NB0), slice(NA + NB0, NM)
CAT = E * R + E
NWT = L // P
LN_EPS, REC_EPS = 1e-5, 1e-7

K_ID, K_BLK, K_MEAN, K_MUL, K_OFF, K_COL = 0, P, 2 * P, 3 * P, 3 * P + NM, 3 * P + 2 * NM
COL_G, COL_H, COL_S, COL_NS, COL_BX, COL_BY, COL_HALF, COL_BQ, COL_EPS = range(9)
K_ALL = K_COL + 9

ROUND = 12582912.0
TWO_PI = 6.28318500518798828125
INV_TWO_PI = 0.15915494309189535
Q_NORM = 10
LOG2E, LN2_HI, LN2_LO = 1.4426950408889634, 0.693359375, -2.12194440054690583e-4


P_ARGS = 20


def constants():
    import numpy as np

    k = np.zeros((P, K_ALL), np.float32)
    row = np.arange(P)
    k[:, K_ID:K_ID + P] = np.eye(P)
    k[:, K_BLK:K_BLK + P] = row[:, None] // 32 == row[None, :] // 32
    k[:, K_MEAN:K_MEAN + P] = 1.0 / L
    a, b0, b1 = np.arange(NA), np.arange(NB0), np.arange(NB1)
    k[:, K_MUL:K_MUL + NM] = np.concatenate([P * a, b0, NB0 * b1])
    k[:, K_OFF:K_OFF + NM] = np.concatenate(
        [np.full(NA, P * (NA - 1)), np.full(NB0, NB0 - 1), np.full(NB1, NB0 * (NB1 - 1))])
    top = row < N
    half_pi, two_pi = np.pi / 2, TWO_PI
    for col, up, down in ((COL_G, -1, 1), (COL_H, 1, -1), (COL_S, -two_pi, two_pi), (COL_NS, two_pi, -two_pi),
                          (COL_BX, half_pi, 0), (COL_BY, 0, -half_pi), (COL_HALF, half_pi, half_pi),
                          (COL_BQ, 0, half_pi), (COL_EPS, LN_EPS, LN_EPS)):
        k[:, K_COL + col] = np.where(top, up, down)
    return k


def build_vit_tower(nc, x, log_dt, lam, w_attn, mask, w_base, b_base, w_router, b_router, lora_a, lora_b,
                    consts, out):
    F, FR, I32, BF = mybir.dt.float32, mybir.dt.float32r, mybir.dt.int32, mybir.dt.bfloat16
    ALU, ACT, AX = mybir.AluOpType, mybir.ActivationFunctionType, mybir.AxisListType

    with ExitStack() as ctx:
        def sb(name, shape, dt=F):
            return ctx.enter_context(nc.sbuf_tensor(name, shape, dt))

        def sb_twice(raw_name, raw_shape, raw_dt, name, shape):
            with nc.sbuf_tensor(raw_name, raw_shape, raw_dt) as raw:
                pass
            return raw, sb(name, shape, FR)

        def ps(name, shape):
            return ctx.enter_context(nc.psum_tensor(name, shape, F))

        def sem(name):
            return ctx.enter_context(nc.semaphore(name))

        wa_raw, wa_lo = sb_twice("wa_raw", [P, NWT, L], F, "wa_lo", [P, NWT, KC, P])
        wb_raw, wb_lo = sb_twice("wb_raw", [P, NWT, L], F, "wb_lo", [P, NWT, KC, P])
        mask_raw, wb_hi = sb_twice("mask_raw", [P, NWT, L], I32, "wb_hi", [P, NWT, KC, P])
        wa_hi = sb("wa_hi", [P, NWT, KC, P], FR)
        wr_raw, wr = sb_twice("wr_raw", [P, KC, 2, CAT], F, "wr", [P, KC, 2, CAT])
        lb_raw, lb_lo = sb_twice("lb_raw", [P, L], F, "lb_lo", [P, L])
        lb_hi = sb("lb_hi", [P, L], FR)
        bias = sb("bias", [P, L])
        bias_r = sb("bias_r", [P, E])
        kst = sb("kst", [P, K_ALL])
        lam_sb = sb("lam_sb", [P, 2])
        dec, turn = sb("dec", [P, H]), sb("turn", [P, H])
        qr, qi = sb("qr", [P, H]), sb("qi", [P, H])
        mul = sb("mul", [P, NM])
        gt, neg_gt, flip = sb("gt", [P, 1]), sb("neg_gt", [P, 1]), sb("flip", [P, 1])
        xn = sb("xn", [P, N, 2])
        xd = sb("xd", [P, 2, 2, N])
        u_t, er_t = sb("u_t", [P, HT, NM]), sb("er_t", [P, HT, NM])
        gh_t = sb("gh_t", [P, 2, HT, NA + NB0])
        g_t, h_t = gh_t[:, 0], gh_t[:, 1]
        k_t = gh_t[:, :, :, :].rearrange("p i h m -> p (i h m)")[:, 0:HT * NM].rearrange("p (h m) -> p h m", h=HT)
        a_t = sb("a_t", [P, HT, NB1])
        xy, pp, qq = sb("xy", [P, 2, HT, NA]), sb("pp", [P, 2, HT, NB1]), sb("qq", [P, 2, HT, NB0])
        t1, t2 = sb("t1", [P, 2, HT, NA]), sb("t2", [P, 2, HT, NA])
        u12 = sb("u12", [P, 2, HT, NA])
        v_sb = sb("v_sb", [P, HT, NA, C])
        b_sb = sb("b_sb", [P, HT, NB1, NB0])
        tmp = sb("tmp", [P, L])
        x1_hi, x1_lo = sb("x1_hi", [P, KC, P], FR), sb("x1_lo", [P, KC, P], FR)
        x2_hi, x2_lo = sb("x2_hi", [P, KC, P], FR), sb("x2_lo", [P, KC, P], FR)
        h1 = sb("h1", [P, L])
        h2 = [sb(f"h2_{i}", [P, L]) for i in range(2)]
        junk = sb("junk", [P, L], BF)
        hw_sb = sb("hw_sb", [P, E, R])
        hw_hi, hw_lo = sb("hw_hi", [P, P], FR), sb("hw_lo", [P, P], FR)
        st1, st2 = sb("st1", [P, 8]), sb("st2", [P, 2, 8])
        gate = sb("gate", [P, 2, E, E])
        gs, tau = sb("gs", [P, 6, E]), sb("tau", [P, 1])
        cat = sb("cat", [P, CAT])
        wb_sum, wb_neg = sb("wb_sum", [P, NWT]), sb("wb_neg", [P, NWT])
        wa_sum, wa_neg = sb("wa_sum", [P, NWT]), sb("wa_neg", [P, NWT])
        mask_sum = sb("mask_sum", [P, NWT, L // 32])

        acc_a = ps("acc_a", [P, L])
        acc_b = ps("acc_b", [P, L])
        turnp = ps("turnp", [P, L])
        small = ps("small", [P, HALF])
        xps = ps("xps", [P, HALF])

        consts_in, params_in, bias_in, lora_in, lorb_in, rt_in, x_in = (sem(n) for n in (
            "consts_in", "params_in", "bias_in", "lora_in", "lorb_in", "rt_in", "x_in"))
        wa_in = [sem(f"wa_in{j}") for j in range(NWT)]
        wb_in = [sem(f"wb_in{j}") for j in range(NWT)]
        mask_in = [sem(f"mask_in{j}") for j in range(NWT)]
        out_stored = [sem("out_stored0"), sem("out_stored1")]
        pstep, halfstep, qstep, q_reciprocal, q_ready = (sem(n) for n in (
            "pstep", "halfstep", "qstep", "q_reciprocal", "q_ready"))
        mask_summed, blk_ready = sem("mask_summed"), sem("blk_ready")
        wa_masked, wa_mean, wa_centred, wa_t, wa_high, wa_copied, wa_low, wa_low_direct, wa_mean_last, wa_centred_last = (sem(n) for n in (
            "wa_masked", "wa_mean", "wa_centred", "wa_t", "wa_high", "wa_copied", "wa_low", "wa_low_direct",
            "wa_mean_last", "wa_centred_last"))
        wb_summed, wb_mean, wb_centred, wb_t, wb_high, wb_low = (sem(n) for n in (
            "wb_summed", "wb_mean", "wb_centred", "wb_t", "wb_high", "wb_low"))
        rt_t, rt_copied, cat_mean, cat_centred, cat_hi, cat_lo = (sem(n) for n in (
            "rt_t", "rt_copied", "cat_mean", "cat_centred", "cat_hi", "cat_lo"))
        lorb_hi, lorb_lo = sem("lorb_hi"), sem("lorb_lo")
        x_twice, w_ready, tab_chain, tab_exponent, tab_phase, tab_exp, tab_sin = (sem(n) for n in (
            "x_twice", "w_ready", "tab_chain", "tab_exponent", "tab_phase", "tab_exp", "tab_sin"))
        v_chain, b_chain, v_ready, b_ready = sem("v_chain"), sem("b_chain"), sem("v_ready"), sem("b_ready")
        kt_ready, kt_hi, kt_copied, kt_lo, h1_ready, h1_copied, h1_stat, h1_dev = (sem(n) for n in (
            "kt_ready", "kt_hi", "kt_copied", "kt_lo", "h1_ready", "h1_copied", "h1_stat", "h1_dev"))
        attn_ready, rs1_chain, h2_ready, h2_stat, h2_dev, rs2_chain = (sem(n) for n in (
            "attn_ready", "rs1_chain", "h2_ready", "h2_stat", "h2_dev", "rs2_chain"))
        h2t_ready, h2t_hi, h2t_lo, cat_ready, gate_chain, hw_ready = (sem(n) for n in (
            "h2t_ready", "h2t_hi", "h2t_lo", "cat_ready", "gate_chain", "hw_ready"))
        hwt_ready, hwt_hi, hwt_lo, ffn_ready, bias_added, out_ready = (sem(n) for n in (
            "hwt_ready", "hwt_hi", "hwt_lo", "ffn_ready", "bias_added", "out_ready"))

        ident = kst[:, K_ID:K_ID + P]

        def col(i):
            return kst[:, K_COL + i:K_COL + i + 1]

        flat = lambda b: b[:, :, :, :].rearrange("p x y z -> p (x y z)")
        wa_rows = [wa_raw[:, j, :] for j in range(NWT)]
        wb_rows = [wb_raw[:, j, :] for j in range(NWT)]
        mask_rows = [mask_raw[:, j, :] for j in range(NWT)]
        rt_rows = E * KC
        rt_stage = hw_sb[0:rt_rows, :, :].rearrange("p e r -> p (e r)")
        cat_raw = wr_raw[:, :, 1, :]
        slot = [b[:, 2 * H * i:2 * H * (i + 1)] for b in (flat(b_sb), tmp) for i in range(4)]

        def block_bank(j):
            bank = acc_a[:, HALF:L] if j % 2 else acc_a[:, 0:HALF] if j < NWT // 2 else small
            return bank[:, 0:L // 32]

        CENTRE_LAST = 4
        DIRECT = 4
        HK = KC // 2
        def raw_half(i):
            return wa_raw[:, i // 2, (i % 2) * HALF:(i % 2 + 1) * HALF]

        LATE = 12

        def half_bank(i, acc=acc_b):
            return acc[:, (i % 2) * HALF:(i % 2 + 1) * HALF]

        def wb_bank(i):
            return half_bank(i, acc_b if i < LATE else acc_a)

        def half_of(w, i):
            return w[:, i // 2, (i % 2) * HK:(i % 2 + 1) * HK, :].rearrange("p k n -> p (k n)")

        kt_full = flat(b_sb).rearrange("p (k n) -> p k n", k=KC)

        x_v = x.rearrange("c (t h) n r -> t h c (n r)", h=HT)
        out_v = out.rearrange("c (t h) l -> t h c l", h=HT)
        lora_v = lora_a.rearrange("e (k p) r -> k p e r", p=P)

        LOOP = range(3, TILES - 3)
        FRONT, BACK = range(1, LOOP.start), range(LOOP.stop, TILES + 1)

        def steps(eng, step):
            for t in FRONT:
                step(t, t % 2)
            with eng.Fori(0, len(LOOP) // 2) as i:
                for u in range(2):
                    step(i * 2 + (LOOP.start + u), (LOOP.start + u) % 2)
            for t in BACK:
                step(t, t % 2)

        def whole(b):
            return b[:, :, :, :]

        def b_factors(i):
            return (pp[:, i].unsqueeze(3).to_broadcast([P, HT, NB1, NB0]),
                    qq[:, i].unsqueeze(2).to_broadcast([P, HT, NB1, NB0]))

        def b_terms(b):
            return b[:, :].rearrange("p (h x y) -> p h x y", h=HT, x=NB1)

        def real(t):
            return not isinstance(t, int) or 0 <= t < TILES

        def later(t, first):
            return not isinstance(t, int) or t >= first

        def at(t, n):
            return isinstance(t, int) and t == n

        def x2_of(t):
            return (x1_hi, x1_lo) if at(t, TILES - 1) else (x2_hi, x2_lo)

        block = ctx.enter_context(nc.Block())

        @block.sync
        def _(sp):
            def load_x(t):
                if later(t, 1):
                    sp.wait_ge(x_twice, t)
                sp.dma_start(xn[:, :, :].rearrange("p n r -> p (n r)"), x_v[t]).then_inc(x_in, 16)

            sp.dma_start(slot[4], log_dt.rearrange("h r -> (h r)").partition_broadcast(P)).then_inc(params_in, 16)
            sp.dma_start(lam_sb[0:N, :], lam).then_inc(params_in, 16)
            sp.dma_start(lam_sb[N:P, :], lam).then_inc(params_in, 16)
            sp.dma_start(kst[:, :], consts).then_inc(consts_in, 16)

            for j in range(NWT):
                sp.dma_start(mask_rows[j], mask[j * P:(j + 1) * P, :]).then_inc(mask_in[j], 16)
                sp.dma_start(wa_rows[j], w_attn[j * P:(j + 1) * P, :]).then_inc(wa_in[j], 16)
                if j == 1:
                    load_x(0)
                    sp.dma_start(rt_stage, w_router.rearrange("e (k p) -> (e k) p", p=P)).then_inc(rt_in, 16)
            for j in range(NWT):
                sp.dma_start(wb_rows[j], w_base[j * P:(j + 1) * P, :]).then_inc(wb_in[j], 16)
                if j == 3:
                    load_x(1)
            for k in range(KC):
                sp.dma_start(cat_raw[:, k, 0:E * R].rearrange("p (e r) -> p e r", e=E), lora_v[k]).then_inc(lora_in, 16)
            sp.dma_start(lb_raw[:, :], lora_b.rearrange("e r l -> (e r) l")).then_inc(lorb_in, 16)
            sp.dma_start(bias[:, :], b_base.partition_broadcast(P)).then_inc(bias_in, 16)
            sp.dma_start(bias_r[:, :], b_router.partition_broadcast(P)).then_inc(bias_in, 16)
            load_x(2)
            load_x(3)

            def step(t, par):
                if real(t + 3):
                    load_x(t + 3)
                if real(t - 1):
                    sp.wait_ge(out_ready, t)
                    sp.dma_start(out_v[t - 1], h2[1 - par][:, :]).then_inc(out_stored[1 - par], 16)

            steps(sp, step)
            sp.wait_ge(out_stored[0], 8 * TILES)
            sp.wait_ge(out_stored[1], 8 * TILES)

        @block.tensor
        def _(pe):
            def block_sums(j):
                pe.wait_ge(mask_summed, j + 1)
                if j >= 2:
                    pe.wait_ge(wa_masked, j - 1)
                pe.matmul(block_bank(j), kst[:, K_BLK:K_BLK + P], mask_sum[:, j, :],
                          start=True, stop=True).then_inc(blk_ready, 1)

            def wa_transposes(j):
                if j < CENTRE_LAST:
                    pe.wait_ge(wa_centred, j + 1)
                else:
                    pe.wait_ge(wa_centred_last, j + 1 - CENTRE_LAST)
                for i in (2 * j, 2 * j + 1):
                    if i >= 2:
                        pe.wait_ge(wa_high, i - 1)
                        if i - 2 < 2 * DIRECT:
                            pe.wait_ge(wa_copied, i - 1)
                        else:
                            pe.wait_ge(wa_low_direct, i - 1 - 2 * DIRECT)
                    for k in range(HK):
                        c = (i % 2 * HK + k) * P
                        mm = pe.transpose(half_bank(i)[:, k * P:(k + 1) * P], wa_rows[j][:, c:c + P], ident)
                    mm.then_inc(wa_t, 1)

            def wb_half(i):
                j = i // 2
                pe.wait_ge(wb_centred, j + 1)
                if i in (LATE, LATE + 1):
                    pe.wait_ge(h2_ready, 2)
                elif i >= 2:
                    pe.wait_ge(wb_high, i - 1)
                    pe.wait_ge(wb_low, i - 1)
                else:
                    pe.wait_ge(wa_high, 2 * NWT)
                    pe.wait_ge(wa_low_direct, 2 * (NWT - DIRECT))
                for k in range(HK):
                    c = (i % 2 * HK + k) * P
                    mm = pe.transpose(wb_bank(i)[:, k * P:(k + 1) * P], wb_rows[j][:, c:c + P], ident)
                mm.then_inc(wb_t, 1)

            def x_transposes(t):
                pe.wait_ge(x_twice, t + 1)
                if later(t, 1):
                    pe.wait_ge(v_ready, t)
                for r in range(2):
                    mm = pe.transpose(xps[:, r * P:(r + 1) * P], xd[:, r, :, :].rearrange("p d n -> p (d n)"), ident)
                mm.then_inc(w_ready, 1)

            def k_transposed(t):
                pe.wait_ge(v_ready, t + 1)
                pe.wait_ge(b_ready, t + 1)
                for h in range(HT):
                    mm = pe.matmul(turnp[:, h * P:(h + 1) * P], b_sb[:, h, :, :].rearrange("p x y -> p (x y)"),
                                   v_sb[:, h, :, :].rearrange("p a c -> p (a c)"), start=True, stop=True)
                mm.then_inc(kt_ready, 1)

            def k_rows(t):
                pe.wait_ge(kt_hi, t + 1)
                pe.wait_ge(kt_copied, t + 1)
                for k in range(KC):
                    mm = pe.transpose(turnp[:, k * P:(k + 1) * P], kt_full[:, k, :], ident)
                mm.then_inc(h1_ready, 1)

            def h2_transposes(t, par):
                pe.wait_ge(h2_ready, t + 1)
                for k in range(KC):
                    mm = pe.transpose(turnp[:, k * P:(k + 1) * P], h2[par][:, k * P:(k + 1) * P], ident)
                mm.then_inc(h2t_ready, 1)

            def product_part(acc, n, a, w, k, first, last):
                cols = acc[:, n * HALF:(n + 1) * HALF].rearrange("p (j n) -> p j n", n=P)
                rows = w[:, n * HK:(n + 1) * HK, k, :] if k is not None else \
                    w[:, n * HALF:(n + 1) * HALF].rearrange("p (j n) -> p j n", n=P)
                return pe.matmul(cols, a, rows, start=first, stop=last)

            def product(acc, hi, lo, w_hi, w_lo, k, first, last, halves=(0, 1)):
                for a, w in ((hi, w_hi), (hi, w_lo), (lo, w_hi)):
                    for n in halves:
                        mm = product_part(acc, n, a, w, k, first and a is hi and w is w_hi, last and a is lo)
                return mm

            def cat_means():
                pe.wait_ge(rt_copied, 1)
                pe.wait_ge(lora_in, 16 * KC)
                for k in range(KC):
                    mm = pe.matmul(small[:, 0:CAT], kst[:, K_MEAN:K_MEAN + P], cat_raw[:, k, :],
                                   start=k == 0, stop=k == KC - 1)
                mm.then_inc(cat_mean, 1)

            def first_attention(n, chunks):
                for k in chunks:
                    mm = product(acc_a, x1_hi[:, k, :], x1_lo[:, k, :], wa_hi, wa_lo, k, k == 0, k == KC - 1, (n,))
                    if n == 1 and k == KC - 1:
                        mm.then_inc(attn_ready, 1)
                    if n == 1 and k >= HK:
                        wb_half(k - HK)

            def step(t, par):
                x2 = x2_of(t - 1)
                if real(t - 1) and real(t):
                    pe.wait_ge(h1_copied, t + 1)
                    h2_transposes(t - 1, 1 - par)
                if real(t):
                    pe.wait_ge(kt_lo, t + 1)
                    for k in range(KC):
                        mm = product(acc_a, x1_hi[:, k, :], x1_lo[:, k, :], wa_hi, wa_lo, k, k == 0, k == KC - 1)
                        if k == KC - 1:
                            mm.then_inc(attn_ready, 1)
                        if at(t, 1) and k in (2, 3, 5, 6):
                            wb_half((2, 3, 5, 6).index(k) + 6)
                        if at(t, 1) and k == 6:
                            cat_means()
                        if at(t, 1) and k == 7:
                            wb_half(10)
                if real(t - 1):
                    pe.wait_ge(h2t_lo, t)
                if real(t + 1):
                    k_transposed(t + 1)
                if at(t, 1):
                    wb_half(11)
                    pe.wait_ge(wb_high, 12)
                    pe.wait_ge(wb_low, 12)
                    for k in range(KC):
                        product(acc_b, x2[0][:, k, :], x2[1][:, k, :], wb_hi, wb_lo, k, k == 0, False, (0,))
                        if k % 2:
                            wb_half(LATE + k // 2)
                if real(t - 1):
                    if at(t, 1):
                        pe.wait_ge(cat_lo, 1)
                    if later(t, 2):
                        pe.wait_ge(hwt_lo, t - 1)
                    for k in range(KC):
                        pe.matmul(small[:, 0:2 * CAT], x2[0][:, k, :], wr[:, k, :, :].rearrange("p s n -> p (s n)"),
                                  start=k == 0, stop=False)
                        mm = pe.matmul(small[:, 0:CAT], x2[1][:, k, :], wr[:, k, 0, :], start=False, stop=k == KC - 1)
                    mm.then_inc(cat_ready, 1)
                    if later(t, 2):
                        pe.wait_ge(out_ready, t - 1)
                    if at(t, 1):
                        pe.wait_ge(wb_high, 2 * NWT)
                        pe.wait_ge(wb_low, 2 * NWT)
                for k in range(KC):
                    if k == 2 and real(t + 2):
                        x_transposes(t + 2)
                    if k == KC // 2 and real(t + 1):
                        k_rows(t + 1)
                    if k == KC // 2 and at(t, TILES - 1):
                        h2_transposes(t, par)
                    if k == KC - 2 and real(t - 1):
                        pe.wait_ge(hw_ready, t)
                        pe.transpose(small[:, 0:P], hw_sb[:, :, :].rearrange("p e r -> p (e r)"), ident)\
                            .then_inc(hwt_ready, 1)
                    if real(t - 1):
                        product(acc_b, x2[0][:, k, :], x2[1][:, k, :], wb_hi, wb_lo, k, k == 0, False,
                                (1,) if at(t, 1) else (0, 1))
                if real(t - 1):
                    if at(t, 1):
                        pe.wait_ge(lorb_lo, 1)
                    pe.wait_ge(hwt_lo, t)
                    product(acc_b, hw_hi[:, :], hw_lo[:, :], lb_hi, lb_lo, None, False, True)\
                        .then_inc(ffn_ready, 1)

            pe.wait_ge(consts_in, 16)
            x_transposes(0)
            block_sums(0)
            block_sums(1)
            wa_transposes(0)
            block_sums(2)
            wa_transposes(1)
            block_sums(3)
            wa_transposes(2)
            block_sums(4)
            wa_transposes(3)
            k_transposed(0)
            block_sums(5)
            wa_transposes(4)
            k_rows(0)
            block_sums(6)
            wa_transposes(5)
            block_sums(7)
            pe.wait_ge(kt_lo, 1)
            pe.wait_ge(wa_high, NWT)
            pe.wait_ge(wa_low, NWT // 2)
            first_attention(0, range(0, 1))
            wa_transposes(6)
            x_transposes(1)
            first_attention(0, range(1, 4))
            wa_transposes(7)
            first_attention(0, range(4, KC))
            pe.wait_ge(rt_in, 16)
            pe.transpose(small[:, HALF - rt_rows:HALF], rt_stage, ident[0:rt_rows, 0:rt_rows]).then_inc(rt_t, 1)
            pe.wait_ge(wa_high, 2 * NWT)
            pe.wait_ge(wa_low, DIRECT)
            pe.wait_ge(wa_low_direct, 2 * (NWT - DIRECT))
            first_attention(1, range(KC))
            pe.wait_ge(h1_copied, 1)
            k_transposed(1)
            wb_half(4)
            wb_half(5)
            x_transposes(2)
            k_rows(1)
            steps(pe, step)

        @block.scalar
        def _(act):
            def wa_centre(j):
                act.wait_ge(wa_masked, j + 1)
                act.activation(wa_neg[:, j:j + 1], wa_sum[:, j:j + 1], ACT.Copy, scale=-1.0 / L).then_inc(wa_mean, 1)
                act.wait_ge(wa_mean, j + 1)
                act.activation(wa_rows[j], wa_rows[j], ACT.Identity, bias=wa_neg[:, j:j + 1]).then_inc(wa_centred, 1)

            def wa_copies(j):
                for i in (2 * j, 2 * j + 1):
                    act.wait_ge(wa_t, i + 1)
                    act.activation(half_of(wa_hi, i), half_bank(i), ACT.Copy).then_inc(wa_high, 1)
                    if j < DIRECT:
                        act.activation(raw_half(i), half_bank(i), ACT.Copy).then_inc(wa_copied, 1)

            def wb_sums(j):
                act.wait_ge(wb_in[j], 16)
                act.activation(junk[:, :], wb_rows[j], ACT.Copy, accum_out=wb_sum[:, j:j + 1]).then_inc(wb_summed, 1)
                act.wait_ge(wb_summed, j + 1)
                act.activation(wb_neg[:, j:j + 1], wb_sum[:, j:j + 1], ACT.Copy, scale=-1.0 / L).then_inc(wb_mean, 1)

            def wb_highs(i):
                act.wait_ge(wb_t, i + 1)
                if i == 0:
                    act.wait_ge(mask_summed, NWT)
                act.activation(half_of(wb_hi, i), wb_bank(i), ACT.Copy).then_inc(wb_high, 1)

            def x_rows_twice(t):
                act.wait_ge(x_in, t * 16 + 16)
                if later(t, 1):
                    act.wait_ge(w_ready, t)
                for r in range(2):
                    op = act.activation(xd[:, r, :, :], xn[:, :, r].unsqueeze(1).to_broadcast([P, 2, N]), ACT.Copy)
                op.then_inc(x_twice, 1)

            def exp_and_sin(t):
                act.wait_ge(tab_exponent, t + 1)
                if later(t, 1):
                    act.wait_ge(b_ready, t)
                act.activation(er_t[:, :, :], er_t[:, :, :], ACT.Exp).then_inc(tab_exp, 1)
                act.wait_ge(tab_phase, t + 1)
                g_a, g_b0 = g_t[:, :, 0:NA], g_t[:, :, NA:NA + NB0]
                h_a, h_b0 = h_t[:, :, 0:NA], h_t[:, :, NA:NA + NB0]
                act.activation(xy[:, 0], g_a, ACT.Sin, scale=-TWO_PI, bias=col(COL_BX))
                act.activation(xy[:, 1], h_a, ACT.Sin, scale=col(COL_S), bias=col(COL_BY))
                act.activation(pp[:, 0], a_t[:, :, :], ACT.Sin, scale=-TWO_PI, bias=col(COL_HALF))
                act.activation(pp[:, 1], u_t[:, :, SB1], ACT.Sin, scale=col(COL_S))
                act.activation(qq[:, 0], g_b0, ACT.Sin, scale=col(COL_S), bias=col(COL_BX))
                act.activation(qq[:, 1], h_b0, ACT.Sin, scale=col(COL_NS), bias=col(COL_BQ))\
                    .then_inc(tab_sin, 1)

            def k_high(t):
                by_head = turnp[:, :].rearrange("p (h a c) -> p h a c", h=HT, a=NA)
                act.wait_ge(kt_ready, t + 1)
                act.activation(kt_full.rearrange("p a (h c) -> p h a c", c=C), by_head, ACT.Copy).then_inc(kt_copied, 1)
                if later(t, 1):
                    act.wait_ge(attn_ready, t)
                act.activation(x1_hi[:, :, :].rearrange("p a (h c) -> p h a c", c=C), by_head, ACT.Copy)\
                    .then_inc(kt_hi, 1)

            def deviation(s, src, stat, dev, t):
                act.activation(s[:, 1:2], s[:, 0:1], ACT.Copy, scale=-1.0 / L).then_inc(stat, 1)
                act.wait_ge(stat, t * 2 + 1)
                act.activation(junk[:, :], src, ACT.Square, bias=s[:, 1:2], accum_out=s[:, 2:3]).then_inc(stat, 1)
                act.wait_ge(stat, t * 2 + 2)
                act.activation(s[:, 3:4], s[:, 2:3], ACT.Sqrt, scale=1.0 / L, bias=col(COL_EPS)).then_inc(dev, 1)

            def h2_deviation(t, par):
                act.wait_ge(h2_ready, t + 1)
                deviation(st2[:, par, :], h2[par][:, :], h2_stat, h2_dev, t)

            def k_copy(t):
                act.wait_ge(h1_ready, t + 1)
                if later(t, 1):
                    act.wait_ge(h2_ready, t)
                act.activation(h1[:, :], turnp[:, :], ACT.Copy, accum_out=st1[:, 0:1]).then_inc(h1_copied, 1)

            def k_deviation(t):
                act.wait_ge(h1_copied, t + 1)
                deviation(st1, h1[:, :], h1_stat, h1_dev, t)

            def step(t, par):
                if real(t - 1):
                    act.wait_ge(h2t_ready, t)
                    if at(t, TILES):
                        act.wait_ge(attn_ready, t)
                    elif later(t, 2):
                        act.wait_ge(ffn_ready, t - 1)
                    act.activation(x2_of(t - 1)[0][:, :, :].rearrange("p k n -> p (k n)"), turnp[:, :], ACT.Copy)\
                        .then_inc(h2t_hi, 1)
                if at(t, 1):
                    wb_sums(7)
                    exp_and_sin(2)
                    wb_highs(6)
                    wb_highs(7)
                    wb_highs(8)
                    wb_highs(9)
                    k_deviation(1)
                    wb_highs(10)
                    wb_highs(11)
                    h2_deviation(0, 0)
                    k_high(2)
                    act.wait_ge(lorb_in, 16)
                    act.activation(lb_hi[:, :], lb_raw[:, :], ACT.Copy).then_inc(lorb_hi, 1)
                    act.wait_ge(cat_centred, 1)
                    act.activation(wr[:, :, 0, :], cat_raw, ACT.Copy).then_inc(cat_hi, 1)
                    for i in range(LATE, 2 * NWT):
                        wb_highs(i)
                if real(t + 2):
                    x_rows_twice(t + 2)
                    exp_and_sin(t + 2)
                if real(t + 1) and later(t, 2):
                    k_high(t + 1)
                if real(t) and later(t, 2):
                    h2_deviation(t, par)
                if real(t + 1):
                    k_copy(t + 1)
                    if later(t, 2):
                        k_deviation(t + 1)
                if real(t - 1):
                    act.wait_ge(hwt_ready, t)
                    act.activation(hw_hi[:, :], small[:, 0:P], ACT.Copy).then_inc(hwt_hi, 1)
                if at(t, 1):
                    h2_deviation(1, 1)
                    k_deviation(2)

            act.wait_ge(consts_in, 16)
            act.wait_ge(pstep, P_ARGS)
            act.activation(slot[5], slot[1], ACT.Tanh, scale=0.5)
            act.activation(slot[6], slot[2], ACT.Sin, scale=TWO_PI)
            act.activation(slot[7], slot[2], ACT.Sin, scale=TWO_PI / 2).then_inc(halfstep, 1)
            x_rows_twice(0)
            exp_and_sin(0)
            wa_centre(0)
            wa_centre(1)
            wa_copies(0)
            wa_centre(2)
            wa_copies(1)
            wa_centre(3)
            wa_copies(2)
            wa_copies(3)
            exp_and_sin(1)
            k_high(0)
            x_rows_twice(1)
            wa_copies(4)
            wa_copies(5)
            k_copy(0)
            k_deviation(0)
            wa_copies(6)
            wb_sums(0)
            wa_copies(7)
            wb_sums(1)
            x_rows_twice(2)
            wb_sums(2)
            wb_sums(3)
            wb_sums(4)
            wb_highs(0)
            wb_highs(1)
            wb_highs(2)
            wb_sums(5)
            wb_highs(3)
            wb_sums(6)
            k_high(1)
            wb_highs(4)
            wb_highs(5)
            k_copy(1)
            steps(act, step)

        @block.gpsimd
        def _(pool):
            def parameters():
                n = 0

                def link(op):
                    nonlocal n
                    op.then_inc(qstep, 1)
                    n += 1
                    pool.wait_ge(qstep, n)

                pool.wait_ge(pstep, P_ARGS)
                two = lambda s: s.rearrange("p (s h) -> p s h", s=2)
                lr, li = lam_sb[:, 0:1], lam_sb[:, 1:2]
                pool.wait_ge(halfstep, 1)
                th, s_, sh = slot[5], slot[6], slot[7]
                link(pool.tensor_tensor(sh, sh, sh, ALU.mult))
                pool.tensor_scalar(slot[0], sh, -2.0, 1.0, ALU.mult, ALU.add)
                link(pool.tensor_scalar(sh, sh, 2.0, None, ALU.mult))
                pool.wait_ge(q_reciprocal, 1)
                link(pool.tensor_tensor(th, th, slot[3], ALU.mult))
                pool.tensor_scalar(slot[1], th, 1.0, None, ALU.add)
                link(pool.tensor_tensor(slot[3], th, slot[0], ALU.mult))
                pool.tensor_tensor(slot[3], slot[3], sh, ALU.subtract)
                link(pool.tensor_tensor(s_, slot[1], s_, ALU.mult))
                nr, dr, ni, di = two(slot[3])[:, 0], two(slot[3])[:, 1], two(s_)[:, 0], two(s_)[:, 1]
                d_r, d_i = two(slot[4])[:, 0], two(slot[4])[:, 1]
                w0, w1 = two(slot[0])[:, 0], two(slot[0])[:, 1]
                pool.tensor_scalar(w0, di, li, None, ALU.mult)
                pool.tensor_scalar(w1, di, lr, None, ALU.mult)
                pool.tensor_scalar(d_r, dr, lr, None, ALU.mult)
                link(pool.tensor_scalar(d_i, dr, li, None, ALU.mult))
                pool.tensor_tensor(d_r, d_r, w0, ALU.subtract)
                link(pool.tensor_tensor(d_i, d_i, w1, ALU.add))
                m0, m1 = two(slot[1])[:, 0], two(slot[1])[:, 1]
                pool.tensor_tensor(m0, d_r, d_r, ALU.mult)
                link(pool.tensor_tensor(m1, d_i, d_i, ALU.mult))
                link(pool.tensor_tensor(m0, m0, m1, ALU.add))
                link(pool.tensor_scalar(m0, m0, REC_EPS, None, ALU.add))
                a0, a1 = two(slot[2])[:, 0], two(slot[2])[:, 1]
                b0, b1 = two(slot[5])[:, 0], two(slot[5])[:, 1]
                pool.tensor_tensor(a0, nr, d_r, ALU.mult)
                pool.tensor_tensor(a1, ni, d_i, ALU.mult)
                pool.tensor_tensor(b0, ni, d_r, ALU.mult)
                link(pool.tensor_tensor(b1, nr, d_i, ALU.mult))
                pool.tensor_tensor(a0, a0, a1, ALU.add)
                link(pool.tensor_tensor(b0, b0, b1, ALU.subtract))
                pool.wait_ge(q_reciprocal, 2)
                pool.tensor_tensor(qr[:, :], a0, m1, ALU.mult)
                pool.tensor_tensor(qi[:, :], b0, m1, ALU.mult).then_inc(q_ready, 1)

            def table_b(t):
                pool.wait_ge(b_chain, t * 3 + 1)
                if t == 0:
                    pool.wait_ge(q_ready, 1)
                else:
                    pool.wait_ge(h1_ready, t)
                    pool.wait_ge(kt_lo, t)
                pool.tensor_tensor(whole(b_sb), *b_factors(0), ALU.mult).then_inc(b_chain, 1)
                pool.tensor_tensor(b_terms(h2[1]), *b_factors(1), ALU.mult).then_inc(b_chain, 1)
                pool.wait_ge(b_chain, t * 3 + 3)
                pool.tensor_tensor(whole(b_sb), whole(b_sb), b_terms(h2[1]), ALU.add).then_inc(b_ready, 1)

            def wa_centre(j):
                pool.wait_ge(wa_masked, j + 1)
                pool.tensor_scalar(wa_neg[:, j:j + 1], wa_sum[:, j:j + 1], -1.0 / L, 0.0, ALU.mult, ALU.add)\
                    .then_inc(wa_mean_last, 1)
                pool.wait_ge(wa_mean_last, j + 1 - CENTRE_LAST)
                pool.tensor_scalar(wa_rows[j], wa_rows[j], 1.0, wa_neg[:, j:j + 1], ALU.mult, ALU.add)\
                    .then_inc(wa_centred_last, 1)

            def wa_lows(j):
                pool.wait_ge(wa_copied, 2 * j + 2)
                pool.tensor_tensor(wa_lo[:, j], wa_rows[j].rearrange("p (k n) -> p k n", n=P), wa_hi[:, j].bitcast(F),
                                   ALU.subtract).then_inc(wa_low, 1)

            def wb_centre(j):
                pool.wait_ge(wb_mean, j + 1)
                pool.tensor_scalar(wb_rows[j], wb_rows[j], 1.0, wb_neg[:, j:j + 1], ALU.mult, ALU.add)\
                    .then_inc(wb_centred, 1)

            parameters()
            table_b(0)
            wa_lows(0)
            wa_centre(4)
            wa_lows(1)
            wa_centre(5)
            wa_lows(2)
            wa_lows(3)
            wa_centre(6)
            wa_centre(7)
            table_b(1)
            for j in range(NWT):
                wb_centre(j)
            table_b(2)
            pool.wait_ge(lorb_hi, 1)
            pool.tensor_tensor(lb_lo[:, :], lb_raw[:, :], lb_hi[:, :].bitcast(F), ALU.subtract).then_inc(lorb_lo, 1)
            pool.wait_ge(cat_hi, 1)
            pool.tensor_tensor(wr[:, :, 1, :], cat_raw, wr[:, :, 0, :].bitcast(F), ALU.subtract).then_inc(cat_lo, 1)

            def step(t, par):
                if real(t - 1):
                    pool.wait_ge(h2t_ready, t)
                    pool.wait_ge(h2_dev, t)
                    h = h2[1 - par][:, :]
                    pool.tensor_tensor(h, h, bias[:, :], ALU.add).then_inc(bias_added, 1)

            pool.wait_ge(bias_in, 32)
            steps(pool, step)

        @block.vector
        def _(dve):
            def chained(s, base):
                n = [base]

                def link(op):
                    op.then_inc(s, 1)
                    n[0] = n[0] + 1
                    dve.wait_ge(s, n[0])
                return link

            def dve_arguments():
                link = chained(pstep, 0)
                x_, k_, r_, p_, w_ = slot[4], slot[0], slot[1], slot[2], slot[3]
                link(dve.tensor_scalar(k_, x_, LOG2E, ROUND, ALU.mult, ALU.add))
                link(dve.tensor_scalar(k_, k_, ROUND, None, ALU.subtract))
                link(dve.tensor_scalar(k_, k_, -126.0, 127.0, ALU.max, ALU.min))
                link(dve.scalar_tensor_tensor(r_, k_, -LN2_HI, x_, ALU.mult, ALU.add))
                link(dve.scalar_tensor_tensor(r_, k_, -LN2_LO, r_, ALU.mult, ALU.add))
                link(dve.tensor_scalar(w_.bitcast(I32), k_, 127.0, 8388608.0, ALU.add, ALU.mult))
                link(dve.tensor_scalar(p_, r_, 1.0 / 5040, None, ALU.mult))
                for c in (1.0 / 720, 1.0 / 120, 1.0 / 24, 1.0 / 6, 0.5, 1.0):
                    link(dve.scalar_tensor_tensor(p_, p_, c, r_, ALU.add, ALU.mult))
                link(dve.scalar_tensor_tensor(p_, p_, 1.0, w_, ALU.add, ALU.mult))
                dt = p_.rearrange("p (h r) -> p r h", r=2)
                lr, li = lam_sb[:, 0:1], lam_sb[:, 1:2]
                dve.tensor_scalar(dec[:, :], dt[:, 0, :], lr, None, ALU.mult)
                dve.tensor_scalar(gt[:, :], lr, 0.0, None, ALU.is_gt)
                link(dve.tensor_scalar(turn[:, :], dt[:, 1, :], li, None, ALU.mult))
                dve.tensor_scalar(neg_gt[:, :], gt[:, :], -1.0, None, ALU.mult)
                dve.tensor_scalar(flip[:, :], gt[:, :], -2.0, 1.0, ALU.mult, ALU.add)
                link(dve.tensor_scalar(turn[:, :], turn[:, :], INV_TWO_PI, None, ALU.mult))
                dve.scalar_tensor_tensor(mul[:, :], kst[:, K_OFF:K_OFF + NM], neg_gt[:, 0:1], kst[:, K_MUL:K_MUL + NM],
                                         ALU.mult, ALU.add)
                two = lambda s: s.rearrange("p (s h) -> p s h", s=2)
                a_, f_ = slot[1], slot[2]
                dve.tensor_scalar(two(a_)[:, 0], dec[:, :], flip[:, 0:1], None, ALU.mult)
                link(dve.tensor_scalar(two(f_)[:, 0], turn[:, :], flip[:, 0:1], None, ALU.mult))
                dve.tensor_scalar(two(a_)[:, 1], two(a_)[:, 0], float(L), None, ALU.mult)
                link(dve.tensor_scalar(two(f_)[:, 1], two(f_)[:, 0], float(L), None, ALU.mult))
                link(dve.tensor_scalar(slot[3], f_, ROUND, -ROUND, ALU.add, ALU.add))
                link(dve.tensor_tensor(f_, f_, slot[3], ALU.subtract))

            def reciprocal_of_tanh():
                dve.wait_ge(halfstep, 1)
                dve.tensor_scalar(slot[3], slot[5], -0.5, 0.5, ALU.mult, ALU.add).then_inc(pstep, 1)
                dve.wait_ge(pstep, P_ARGS + 1)
                dve.reciprocal(slot[3], slot[3]).then_inc(q_reciprocal, 1)

            def reciprocal_of_norm():
                dve.wait_ge(qstep, Q_NORM)
                dve.reciprocal(slot[1][:, H:2 * H], slot[1][:, 0:H]).then_inc(q_reciprocal, 1)

            def mask_sums(j):
                dve.wait_ge(mask_in[j], 16)
                dve.tensor_reduce(mask_sum[:, j, :], mask_rows[j].rearrange("p (k b) -> p k b", b=32), AX.X, ALU.add)\
                    .then_inc(mask_summed, 1)

            def wa_mask(j):
                dve.wait_ge(blk_ready, j + 1)
                dve.wait_ge(wa_in[j], 16)
                blocks = block_bank(j).unsqueeze(2).to_broadcast([P, L // 32, 32])
                rows = wa_rows[j].rearrange("p (k b) -> p k b", b=32)
                dve.scalar_tensor_tensor(rows, blocks, 0.0, rows, ALU.is_gt, ALU.mult, accum_out=wa_sum[:, j:j + 1])\
                    .then_inc(wa_masked, 1)

            def wa_lows(i):
                dve.wait_ge(wa_high, i + 1)
                dve.tensor_tensor(half_of(wa_lo, i), half_bank(i), half_of(wa_hi, i).bitcast(F), ALU.subtract)\
                    .then_inc(wa_low_direct, 1)

            def wb_lows(i):
                dve.wait_ge(wb_high, i + 1)
                dve.wait_ge(wb_t, i + 1)
                dve.tensor_tensor(half_of(wb_lo, i), wb_bank(i), half_of(wb_hi, i).bitcast(F), ALU.subtract)\
                    .then_inc(wb_low, 1)

            def over_j(v, n):
                return v.unsqueeze(2).to_broadcast([P, HT, n])

            def decay(s, n):
                return er_t[:, :, s].unsqueeze(1).to_broadcast([P, 2, HT, n])

            def phases(t):
                link = chained(tab_chain, t * 3)
                heads = bass.ds(t * HT, HT)
                m = mul[:, :].unsqueeze(1).to_broadcast([P, HT, NM])
                dve.tensor_tensor(er_t[:, :, :], over_j(dec[:, heads], NM), m, ALU.mult).then_inc(tab_exponent, 1)
                link(dve.tensor_tensor(u_t[:, :, :], over_j(turn[:, heads], NM), m, ALU.mult))
                link(dve.tensor_scalar(k_t, u_t[:, :, :], ROUND, -ROUND, ALU.add, ALU.add))
                link(dve.tensor_tensor(u_t[:, :, :], u_t[:, :, :], k_t, ALU.subtract))
                ab = u_t[:, :, 0:NA + NB0]
                dve.scalar_tensor_tensor(g_t, ab, col(COL_G), ab, ALU.mult, ALU.max)
                dve.scalar_tensor_tensor(h_t, ab, col(COL_H), ab, ALU.mult, ALU.max)
                dve.scalar_tensor_tensor(a_t[:, :, :], u_t[:, :, SB1], -1.0, u_t[:, :, SB1], ALU.mult, ALU.max)\
                    .then_inc(tab_phase, 1)

            def table_v(t):
                heads = bass.ds(t * HT, HT)

                def q(v):
                    return v[:, heads].unsqueeze(1).unsqueeze(3).to_broadcast([P, 2, HT, NA])

                def w(r):
                    rows = xps[:, r * P:(r + 1) * P].rearrange("p (h c) -> p h c", c=C)
                    return rows.unsqueeze(2).to_broadcast([P, HT, NA, C])

                def u(i):
                    return u12[:, i].unsqueeze(3).to_broadcast([P, HT, NA, C])

                tmp4 = tmp[:, :].rearrange("p (h a c) -> p h a c", h=HT, a=NA)
                dve.wait_ge(tab_sin, t + 1)
                dve.tensor_tensor(whole(xy), whole(xy), decay(SA, NA), ALU.mult).then_inc(v_chain, 1)
                dve.wait_ge(v_chain, t * 4 + 1)
                dve.tensor_tensor(whole(t1), whole(xy), q(qr), ALU.mult)
                dve.tensor_tensor(whole(t2), whole(xy), q(qi), ALU.mult).then_inc(v_chain, 1)
                dve.wait_ge(v_chain, t * 4 + 2)
                dve.tensor_tensor(u12[:, 0], t1[:, 0], t2[:, 1], ALU.add)
                dve.tensor_tensor(u12[:, 1], t1[:, 1], t2[:, 0], ALU.subtract).then_inc(v_chain, 1)
                dve.wait_ge(w_ready, t + 1)
                if later(t, 1):
                    dve.wait_ge(kt_ready, t)
                    dve.wait_ge(b_ready, t)
                dve.wait_ge(v_chain, t * 4 + 3)
                dve.tensor_tensor(whole(v_sb), w(0), u(0), ALU.mult)
                dve.tensor_tensor(tmp4, w(1), u(1), ALU.mult).then_inc(v_chain, 1)
                dve.wait_ge(v_chain, t * 4 + 4)
                dve.tensor_tensor(whole(v_sb), whole(v_sb), tmp4, ALU.add).then_inc(v_ready, 1)

            def decay_b(t):
                dve.wait_ge(tab_sin, t + 1)
                dve.tensor_tensor(whole(pp), whole(pp), decay(SB1, NB1), ALU.mult)
                dve.tensor_tensor(whole(qq), whole(qq), decay(SB0, NB0), ALU.mult).then_inc(b_chain, 1)

            def table_b(t):
                decay_b(t)
                dve.wait_ge(h1_ready, t)
                dve.wait_ge(kt_lo, t)
                dve.wait_ge(v_ready, t + 1)
                dve.wait_ge(b_chain, t * 3 + 1)
                dve.tensor_tensor(whole(b_sb), *b_factors(0), ALU.mult)
                dve.tensor_tensor(b_terms(tmp), *b_factors(1), ALU.mult).then_inc(b_chain, 2)
                dve.wait_ge(b_chain, t * 3 + 3)
                dve.tensor_tensor(whole(b_sb), whole(b_sb), b_terms(tmp), ALU.add).then_inc(b_ready, 1)

            def k_low(t):
                dve.wait_ge(kt_copied, t + 1)
                dve.wait_ge(kt_hi, t + 1)
                dve.tensor_tensor(x1_lo[:, :, :], kt_full, x1_hi[:, :, :].bitcast(F), ALU.subtract).then_inc(kt_lo, 1)

            def reciprocal_deviation(s, dev, s_chain, t):
                dve.wait_ge(dev, t + 1)
                dve.tensor_scalar(s[:, 4:5], s[:, 2:3], 1.0 / L, LN_EPS, ALU.mult, ALU.add)
                dve.reciprocal(s[:, 5:6], s[:, 3:4]).then_inc(s_chain, 1)
                dve.wait_ge(s_chain, t * 4 + 1)
                dve.scalar_tensor_tensor(s[:, 6:7], s[:, 5:6], s[:, 5:6], s[:, 4:5], ALU.mult, ALU.mult).then_inc(s_chain, 1)
                dve.wait_ge(s_chain, t * 4 + 2)
                dve.tensor_scalar(s[:, 7:8], s[:, 6:7], -0.5, 1.5, ALU.mult, ALU.add).then_inc(s_chain, 1)
                dve.wait_ge(s_chain, t * 4 + 3)
                dve.tensor_tensor(s[:, 4:5], s[:, 5:6], s[:, 7:8], ALU.mult).then_inc(s_chain, 1)

            def attention_residual(t, par):
                dve.wait_ge(attn_ready, t + 1)
                dve.wait_ge(rs1_chain, t * 4 + 4)
                if later(t, 2):
                    dve.wait_ge(out_stored[par], t * 8 - 8 * par)
                dve.scalar_tensor_tensor(h2[par][:, :], acc_a[:, :], st1[:, 4:5], h1[:, :], ALU.mult, ALU.add,
                                         accum_out=st2[:, par, 0:1]).then_inc(h2_ready, 1)

            def gates(t, par):
                link = chained(gate_chain, t * 9)
                z, cnt, tot, inv, cand, w = (gs[:, i, :] for i in range(6))
                z_j = z.unsqueeze(1).to_broadcast([P, E, E])
                z_i = z.unsqueeze(2).to_broadcast([P, E, E])
                dve.wait_ge(cat_ready, t + 1)
                dve.wait_ge(rs2_chain, t * 4 + 4)
                link(dve.tensor_copy(cat[:, :], small[:, CAT:2 * CAT]))
                link(dve.tensor_tensor(cat[:, :], small[:, 0:CAT], cat[:, :], ALU.add))
                link(dve.scalar_tensor_tensor(z, cat[:, E * R:CAT], st2[:, par, 4:5], bias_r[:, :], ALU.mult, ALU.add))
                link(dve.tensor_tensor(gate[:, 0], z_j, z_i, ALU.is_ge))
                dve.tensor_reduce(cnt, gate[:, 0], AX.X, ALU.add)
                link(dve.tensor_tensor(gate[:, 1], gate[:, 0], z_j, ALU.mult))
                dve.reciprocal(inv, cnt)
                link(dve.tensor_reduce(tot, gate[:, 1], AX.X, ALU.add))
                link(dve.scalar_tensor_tensor(cand, tot, -1.0, inv, ALU.add, ALU.mult))
                link(dve.tensor_reduce(tau[:, :], cand, AX.X, ALU.max))
                link(dve.tensor_scalar(w, z, tau[:, 0:1], 0.0, ALU.subtract, ALU.max))
                dve.tensor_tensor(hw_sb[:, :, :], cat[:, 0:E * R].rearrange("p (e r) -> p e r", e=E),
                                  w.unsqueeze(2).to_broadcast([P, E, R]), ALU.mult).then_inc(hw_ready, 1)

            def h2_low(t):
                dve.wait_ge(h2t_hi, t + 1)
                hi, lo = x2_of(t)
                dve.tensor_tensor(lo[:, :, :].rearrange("p k n -> p (k n)"), turnp[:, :],
                                  hi[:, :, :].bitcast(F).rearrange("p k n -> p (k n)"), ALU.subtract)\
                    .then_inc(h2t_lo, 1)

            def step(t, par):
                if real(t - 1):
                    if not at(t, TILES):
                        h2_low(t - 1)
                    if at(t, 1):
                        decay_b(2)
                        wb_lows(6)
                        wb_lows(7)
                        table_v(2)
                        wb_lows(8)
                        wb_lows(9)
                        wb_lows(10)
                        wb_lows(11)
                        reciprocal_deviation(st1, h1_dev, rs1_chain, 1)
                        dve.wait_ge(b_ready, 3)
                        attention_residual(1, 1)
                        dve.wait_ge(cat_mean, 1)
                        dve.tensor_tensor(cat_raw, cat_raw, small[:, 0:CAT].unsqueeze(1).to_broadcast([P, KC, CAT]),
                                          ALU.subtract).then_inc(cat_centred, 1)
                        wb_lows(LATE)
                        phases(3)
                        for i in range(LATE + 1, 2 * NWT):
                            wb_lows(i)
                        dve.wait_ge(bias_in, 32)
                    reciprocal_deviation(st2[:, 1 - par, :], h2_dev, rs2_chain, t - 1)
                if real(t) and later(t, 2):
                    reciprocal_deviation(st1, h1_dev, rs1_chain, t)
                    if real(t + 1):
                        table_b(t + 1)
                if real(t + 2) and later(t, 2):
                    phases(t + 2)
                if real(t) and later(t, 2):
                    attention_residual(t, par)
                if real(t + 1):
                    k_low(t + 1)
                if real(t - 1):
                    gates(t - 1, 1 - par)
                if real(t + 2) and later(t, 2):
                    table_v(t + 2)
                if real(t - 1):
                    dve.wait_ge(hwt_hi, t)
                    dve.tensor_tensor(hw_lo[:, :], small[:, 0:P], hw_hi[:, :].bitcast(F), ALU.subtract).then_inc(hwt_lo, 1)
                    if at(t, 1):
                        table_v(3)
                    if at(t, TILES - 1):
                        h2_low(t)
                    dve.wait_ge(ffn_ready, t)
                    dve.wait_ge(bias_added, t)
                    h = h2[1 - par][:, :]
                    dve.scalar_tensor_tensor(h, acc_b[:, :], st2[:, 1 - par, 4:5], h, ALU.mult, ALU.add).then_inc(out_ready, 1)

            dve.wait_ge(params_in, 48)
            dve.wait_ge(consts_in, 16)
            dve_arguments()
            phases(0)
            mask_sums(0)
            reciprocal_of_tanh()
            mask_sums(1)
            wa_mask(0)
            mask_sums(2)
            wa_mask(1)
            mask_sums(3)
            wa_mask(2)
            decay_b(0)
            reciprocal_of_norm()
            mask_sums(4)
            wa_mask(3)
            dve.wait_ge(q_ready, 1)
            table_v(0)
            phases(1)
            mask_sums(5)
            wa_mask(4)
            mask_sums(6)
            wa_mask(5)
            decay_b(1)
            k_low(0)
            wa_lows(8)
            wa_lows(9)
            mask_sums(7)
            wa_mask(6)
            wa_lows(10)
            wa_lows(11)
            wa_mask(7)
            for i in range(12, 2 * NWT):
                wa_lows(i)
            table_v(1)
            dve.wait_ge(rt_t, 1)
            dve.tensor_copy(cat_raw[:, :, E * R:CAT],
                            small[:, HALF - rt_rows:HALF].rearrange("p (e k) -> p k e", e=E)).then_inc(rt_copied, 1)
            for i in range(4):
                wb_lows(i)
            reciprocal_deviation(st1, h1_dev, rs1_chain, 0)
            attention_residual(0, 0)
            k_low(1)
            phases(2)
            wb_lows(4)
            wb_lows(5)
            steps(dve, step)


_INS = ['x', 'L0_tok_log_dt', 'L0_tok_Lambda', 'L0_attn_weight', 'L0_attn_mask', 'L0_ffn_W_base', 'L0_ffn_b_base',
        'L0_ffn_W_router', 'L0_ffn_b_router', 'L0_ffn_lora_A', 'L0_ffn_lora_B']


def kernel(**inputs):
    import numpy as _np
    import concourse.bacc as _bacc
    from concourse import mybir as _mybir
    from concourse.bass_utils import run_bass_kernel_spmd as _run

    nc = _bacc.Bacc("TRN2", target_bir_lowering=False, num_devices=1)
    arrays, args = {}, []
    for name in _INS:
        arrays[f"in_{name}"] = _np.ascontiguousarray(inputs[name])
    arrays["in_consts"] = constants()
    for name, a in arrays.items():
        args.append(nc.dram_tensor(name, a.shape, _mybir.dt.from_np(a.dtype), kind="ExternalInput").ap())
    out = nc.dram_tensor("out", (C, H, L), _mybir.dt.float32, kind="ExternalOutput").ap()
    build_vit_tower(nc, *args, out)
    return _run(nc, [arrays], core_ids=[0]).results[0]["out"]
```

```python
import concourse.bass as bass
from concourse import mybir
from contextlib import ExitStack


C, H, N, L = 16, 128, 64, 1024
E, R = 8, 16
P = 128
HT = P // C
TILES = H // HT
KC = L // P
HALF = 512
NA, NB1, NB0 = 8, 8, 16
NM = NA + NB0 + NB1
SA, SB0, SB1 = slice(0, NA), slice(NA, NA + NB0), slice(NA + NB0, NM)
CAT = E * R + E
NWT = L // P
LN_EPS, REC_EPS = 1e-5, 1e-7

K_ID, K_BLK, K_MEAN, K_MUL, K_OFF, K_COL = 0, P, 2 * P, 3 * P, 3 * P + NM, 3 * P + 2 * NM
COL_G, COL_H, COL_S, COL_NS, COL_BX, COL_BY, COL_HALF, COL_BQ, COL_EPS = range(9)
K_ALL = K_COL + 9

ROUND = 12582912.0
TWO_PI = 6.28318500518798828125
INV_TWO_PI = 0.15915494309189535
LOG2E, LN2_HI, LN2_LO = 1.4426950408889634, 0.693359375, -2.12194440054690583e-4

P_ARGS = 20
Q_NORM = 10


def constants():
    import numpy as np

    k = np.zeros((P, K_ALL), np.float32)
    row = np.arange(P)
    k[:, K_ID:K_ID + P] = np.eye(P)
    k[:, K_BLK:K_BLK + P] = row[:, None] // 32 == row[None, :] // 32
    k[:, K_MEAN:K_MEAN + P] = 1.0 / L
    a, b0, b1 = np.arange(NA), np.arange(NB0), np.arange(NB1)
    k[:, K_MUL:K_MUL + NM] = np.concatenate([P * a, b0, NB0 * b1])
    k[:, K_OFF:K_OFF + NM] = np.concatenate(
        [np.full(NA, P * (NA - 1)), np.full(NB0, NB0 - 1), np.full(NB1, NB0 * (NB1 - 1))])
    top = row < N
    half_pi, two_pi = np.pi / 2, TWO_PI
    for col, up, down in ((COL_G, -1, 1), (COL_H, 1, -1), (COL_S, -two_pi, two_pi), (COL_NS, two_pi, -two_pi),
                          (COL_BX, half_pi, 0), (COL_BY, 0, -half_pi), (COL_HALF, half_pi, half_pi),
                          (COL_BQ, 0, half_pi), (COL_EPS, LN_EPS, LN_EPS)):
        k[:, K_COL + col] = np.where(top, up, down)
    return k


def build_vit_tower(nc, x, log_dt, lam, w_attn, mask, w_base, b_base, w_router, b_router, lora_a, lora_b,
                    consts, out):
    F, FR, I32, BF = mybir.dt.float32, mybir.dt.float32r, mybir.dt.int32, mybir.dt.bfloat16
    ALU, ACT, AX = mybir.AluOpType, mybir.ActivationFunctionType, mybir.AxisListType

    with ExitStack() as ctx:
        def sb(name, shape, dt=F):
            return ctx.enter_context(nc.sbuf_tensor(name, shape, dt))

        def sb_twice(raw_name, raw_shape, raw_dt, name, shape):
            with nc.sbuf_tensor(raw_name, raw_shape, raw_dt) as raw:
                pass
            return raw, sb(name, shape, FR)

        def ps(name, shape):
            return ctx.enter_context(nc.psum_tensor(name, shape, F))

        def sem(name):
            return ctx.enter_context(nc.semaphore(name))

        wa_raw, wa_lo = sb_twice("wa_raw", [P, NWT, L], F, "wa_lo", [P, NWT, KC, P])
        wb_raw, wb_lo = sb_twice("wb_raw", [P, NWT, L], F, "wb_lo", [P, NWT, KC, P])
        mask_raw, wb_hi = sb_twice("mask_raw", [P, NWT, L], I32, "wb_hi", [P, NWT, KC, P])
        wa_hi = sb("wa_hi", [P, NWT, KC, P], FR)
        wr_raw, wr = sb_twice("wr_raw", [P, KC, 2, CAT], F, "wr", [P, KC, 2, CAT])
        lb_raw, lb_lo = sb_twice("lb_raw", [P, L], F, "lb_lo", [P, L])
        lb_hi = sb("lb_hi", [P, L], FR)
        bias = sb("bias", [P, L])
        bias_r = sb("bias_r", [P, E])
        kst = sb("kst", [P, K_ALL])
        lam_sb = sb("lam_sb", [P, 2])
        dec, turn = sb("dec", [P, H]), sb("turn", [P, H])
        qr, qi = sb("qr", [P, H]), sb("qi", [P, H])
        mul = sb("mul", [P, NM])
        gt, neg_gt, flip = sb("gt", [P, 1]), sb("neg_gt", [P, 1]), sb("flip", [P, 1])
        xn = sb("xn", [P, N, 2])
        xd = sb("xd", [P, 2, 2, N])
        u_t, er_t = sb("u_t", [P, HT, NM]), sb("er_t", [P, HT, NM])
        gh_t = sb("gh_t", [P, 2, HT, NA + NB0])
        g_t, h_t = gh_t[:, 0], gh_t[:, 1]
        k_t = gh_t[:, :, :, :].rearrange("p i h m -> p (i h m)")[:, 0:HT * NM].rearrange("p (h m) -> p h m", h=HT)
        a_t = sb("a_t", [P, HT, NB1])
        xy, pp, qq = sb("xy", [P, 2, HT, NA]), sb("pp", [P, 2, HT, NB1]), sb("qq", [P, 2, HT, NB0])
        t1, t2 = sb("t1", [P, 2, HT, NA]), sb("t2", [P, 2, HT, NA])
        u12 = sb("u12", [P, 2, HT, NA])
        v_sb = sb("v_sb", [P, HT, NA, C])
        b_sb = sb("b_sb", [P, HT, NB1, NB0])
        tmp = sb("tmp", [P, L])
        x1_hi, x1_lo = sb("x1_hi", [P, KC, P], FR), sb("x1_lo", [P, KC, P], FR)
        x2_hi, x2_lo = sb("x2_hi", [P, KC, P], FR), sb("x2_lo", [P, KC, P], FR)
        h1 = sb("h1", [P, L])
        h2 = [sb(f"h2_{i}", [P, L]) for i in range(2)]
        junk = sb("junk", [P, L], BF)
        hw_sb = sb("hw_sb", [P, E, R])
        hw_hi, hw_lo = sb("hw_hi", [P, P], FR), sb("hw_lo", [P, P], FR)
        st1, st2 = sb("st1", [P, 8]), sb("st2", [P, 2, 8])
        gate = sb("gate", [P, 2, E, E])
        gs, tau = sb("gs", [P, 6, E]), sb("tau", [P, 1])
        cat = sb("cat", [P, CAT])
        wb_sum, wb_neg = sb("wb_sum", [P, NWT]), sb("wb_neg", [P, NWT])
        wa_sum, wa_neg = sb("wa_sum", [P, NWT]), sb("wa_neg", [P, NWT])
        mask_sum = sb("mask_sum", [P, NWT, L // 32])

        acc_a = ps("acc_a", [P, L])
        acc_b = ps("acc_b", [P, L])
        turnp = ps("turnp", [P, L])
        small = ps("small", [P, HALF])
        xps = ps("xps", [P, HALF])

        consts_in, params_in, bias_in, lora_in, lorb_in, rt_in, x_in = (sem(n) for n in (
            "consts_in", "params_in", "bias_in", "lora_in", "lorb_in", "rt_in", "x_in"))
        wa_in = [sem(f"wa_in{j}") for j in range(NWT)]
        wb_in = [sem(f"wb_in{j}") for j in range(NWT)]
        mask_in = [sem(f"mask_in{j}") for j in range(NWT)]
        out_stored = [sem("out_stored0"), sem("out_stored1")]
        pstep, halfstep, qstep, q_reciprocal, q_ready = (sem(n) for n in (
            "pstep", "halfstep", "qstep", "q_reciprocal", "q_ready"))
        mask_summed, blk_ready = sem("mask_summed"), sem("blk_ready")
        wa_masked, wa_mean, wa_centred, wa_t, wa_high, wa_copied, wa_low = (sem(n) for n in (
            "wa_masked", "wa_mean", "wa_centred", "wa_t", "wa_high", "wa_copied", "wa_low"))
        wa_low_direct, wa_mean_last, wa_centred_last = (sem(n) for n in (
            "wa_low_direct", "wa_mean_last", "wa_centred_last"))
        wb_summed, wb_mean, wb_centred, wb_t, wb_high, wb_low = (sem(n) for n in (
            "wb_summed", "wb_mean", "wb_centred", "wb_t", "wb_high", "wb_low"))
        rt_t, rt_copied, cat_mean, cat_centred, cat_hi, cat_lo = (sem(n) for n in (
            "rt_t", "rt_copied", "cat_mean", "cat_centred", "cat_hi", "cat_lo"))
        lorb_hi, lorb_lo = sem("lorb_hi"), sem("lorb_lo")
        x_twice, w_ready, tab_chain, tab_exponent, tab_phase, tab_exp, tab_sin = (sem(n) for n in (
            "x_twice", "w_ready", "tab_chain", "tab_exponent", "tab_phase", "tab_exp", "tab_sin"))
        v_chain, b_chain, v_ready, b_ready = sem("v_chain"), sem("b_chain"), sem("v_ready"), sem("b_ready")
        kt_ready, kt_hi, kt_copied, kt_lo, h1_ready, h1_copied, h1_stat, h1_dev = (sem(n) for n in (
            "kt_ready", "kt_hi", "kt_copied", "kt_lo", "h1_ready", "h1_copied", "h1_stat", "h1_dev"))
        attn_ready, rs1_chain, h2_ready, h2_stat, h2_dev, rs2_chain = (sem(n) for n in (
            "attn_ready", "rs1_chain", "h2_ready", "h2_stat", "h2_dev", "rs2_chain"))
        h2t_ready, h2t_hi, h2t_lo, cat_ready, gate_chain, hw_ready = (sem(n) for n in (
            "h2t_ready", "h2t_hi", "h2t_lo", "cat_ready", "gate_chain", "hw_ready"))
        hwt_ready, hwt_hi, hwt_lo, ffn_ready, bias_added, out_ready = (sem(n) for n in (
            "hwt_ready", "hwt_hi", "hwt_lo", "ffn_ready", "bias_added", "out_ready"))

        ident = kst[:, K_ID:K_ID + P]

        def col(i):
            return kst[:, K_COL + i:K_COL + i + 1]

        flat = lambda b: b[:, :, :, :].rearrange("p x y z -> p (x y z)")
        wa_rows = [wa_raw[:, j, :] for j in range(NWT)]
        wb_rows = [wb_raw[:, j, :] for j in range(NWT)]
        mask_rows = [mask_raw[:, j, :] for j in range(NWT)]
        rt_rows = E * KC
        rt_stage = hw_sb[0:rt_rows, :, :].rearrange("p e r -> p (e r)")
        cat_raw = wr_raw[:, :, 1, :]
        slot = [b[:, 2 * H * i:2 * H * (i + 1)] for b in (flat(b_sb), tmp) for i in range(4)]

        def block_bank(j):
            bank = acc_a[:, HALF:L] if j % 2 else acc_a[:, 0:HALF] if j < NWT // 2 else small
            return bank[:, 0:L // 32]

        CENTRE_LAST, DIRECT = NWT // 2 + 1, NWT // 2
        HK = KC // 2
        LATE = 12

        def raw_half(i):
            return wa_raw[:, i // 2, (i % 2) * HALF:(i % 2 + 1) * HALF]

        def half_bank(i, acc=acc_b):
            return acc[:, (i % 2) * HALF:(i % 2 + 1) * HALF]

        def wb_bank(i):
            return half_bank(i, acc_b if i < LATE else acc_a)

        def half_of(w, i):
            return w[:, i // 2, (i % 2) * HK:(i % 2 + 1) * HK, :].rearrange("p k n -> p (k n)")

        kt_full = flat(b_sb).rearrange("p (k n) -> p k n", k=KC)

        x_v = x.rearrange("c (t h) n r -> t h c (n r)", h=HT)
        out_v = out.rearrange("c (t h) l -> t h c l", h=HT)
        lora_v = lora_a.rearrange("e (k p) r -> k p e r", p=P)

        LOOP = range(2, TILES - 4)

        def steps(eng, step):
            with eng.Fori(0, len(LOOP) // 2) as i:
                for u in range(2):
                    step(i * 2 + (LOOP.start + u), (LOOP.start + u) % 2)
            for t in range(LOOP.stop, TILES):
                step(t, t % 2)

        def whole(b):
            return b[:, :, :, :]

        def b_factors(i):
            return (pp[:, i].unsqueeze(3).to_broadcast([P, HT, NB1, NB0]),
                    qq[:, i].unsqueeze(2).to_broadcast([P, HT, NB1, NB0]))

        def b_terms(b):
            return b[:, :].rearrange("p (h x y) -> p h x y", h=HT, x=NB1)

        def real(t):
            return not isinstance(t, int) or 0 <= t < TILES

        def later(t, first):
            return not isinstance(t, int) or t >= first

        def at(t, n):
            return isinstance(t, int) and t == n

        def x2_of(t):
            return (x1_hi, x1_lo) if at(t, TILES - 1) else (x2_hi, x2_lo)

        block = ctx.enter_context(nc.Block())

        @block.sync
        def _(sp):
            def load_x(t):
                if later(t, 1):
                    sp.wait_ge(x_twice, t)
                sp.dma_start(xn[:, :, :].rearrange("p n r -> p (n r)"), x_v[t]).then_inc(x_in, 16)

            sp.dma_start(slot[4], log_dt.rearrange("h r -> (h r)").partition_broadcast(P)).then_inc(params_in, 16)
            sp.dma_start(lam_sb[0:N, :], lam).then_inc(params_in, 16)
            sp.dma_start(lam_sb[N:P, :], lam).then_inc(params_in, 16)
            sp.dma_start(kst[:, :], consts).then_inc(consts_in, 16)

            for j in range(NWT):
                sp.dma_start(mask_rows[j], mask[j * P:(j + 1) * P, :]).then_inc(mask_in[j], 16)
                sp.dma_start(wa_rows[j], w_attn[j * P:(j + 1) * P, :]).then_inc(wa_in[j], 16)
                if j == 1:
                    load_x(0)
                    sp.dma_start(rt_stage, w_router.rearrange("e (k p) -> (e k) p", p=P)).then_inc(rt_in, 16)
            for j in range(NWT):
                sp.dma_start(wb_rows[j], w_base[j * P:(j + 1) * P, :]).then_inc(wb_in[j], 16)
                if j == 3:
                    load_x(1)
            for k in range(KC):
                sp.dma_start(cat_raw[:, k, 0:E * R].rearrange("p (e r) -> p e r", e=E), lora_v[k]).then_inc(lora_in, 16)
            sp.dma_start(lb_raw[:, :], lora_b.rearrange("e r l -> (e r) l")).then_inc(lorb_in, 16)
            sp.dma_start(bias[:, :], b_base.partition_broadcast(P)).then_inc(bias_in, 16)
            sp.dma_start(bias_r[:, :], b_router.partition_broadcast(P)).then_inc(bias_in, 16)
            load_x(2)
            load_x(3)
            load_x(4)

            def store(t, par, cols=slice(0, L)):
                sp.dma_start(out_v[t][:, :, cols], h2[par][:, cols]).then_inc(out_stored[par], 16)

            sp.wait_ge(out_ready, 1)
            store(0, 0)

            def step(t, par):
                if real(t + 3):
                    load_x(t + 3)
                sp.wait_ge(out_ready, t)
                store(t - 1, 1 - par)

            steps(sp, step)
            for n in range(2):
                sp.wait_ge(out_ready, TILES + n)
                store(TILES - 1, 1, slice(n * HALF, (n + 1) * HALF))
            sp.wait_ge(out_stored[0], 8 * TILES)
            sp.wait_ge(out_stored[1], 8 * TILES + 16)

        @block.tensor
        def _(pe):
            def block_sums(j):
                pe.wait_ge(mask_summed, j + 1)
                if j >= 2:
                    pe.wait_ge(wa_masked, j - 1)
                pe.matmul(block_bank(j), kst[:, K_BLK:K_BLK + P], mask_sum[:, j, :],
                          start=True, stop=True).then_inc(blk_ready, 1)

            def wa_transposes(j):
                if j < CENTRE_LAST:
                    pe.wait_ge(wa_centred, j + 1)
                else:
                    pe.wait_ge(wa_centred_last, j + 1 - CENTRE_LAST)
                for i in (2 * j, 2 * j + 1):
                    if i >= 2:
                        pe.wait_ge(wa_high, i - 1)
                        if i - 2 < 2 * DIRECT:
                            pe.wait_ge(wa_copied, i - 1)
                        else:
                            pe.wait_ge(wa_low_direct, i - 1 - 2 * DIRECT)
                    for k in range(HK):
                        c = (i % 2 * HK + k) * P
                        mm = pe.transpose(half_bank(i)[:, k * P:(k + 1) * P], wa_rows[j][:, c:c + P], ident)
                    mm.then_inc(wa_t, 1)

            def wb_half(i):
                j = i // 2
                pe.wait_ge(wb_centred, j + 1)
                if i in (LATE, LATE + 1):
                    pe.wait_ge(h2_ready, 2)
                elif i >= 2:
                    pe.wait_ge(wb_high, i - 1)
                    pe.wait_ge(wb_low, i - 1)
                else:
                    pe.wait_ge(wa_high, 2 * NWT)
                    pe.wait_ge(wa_low_direct, 2 * (NWT - DIRECT))
                for k in range(HK):
                    c = (i % 2 * HK + k) * P
                    mm = pe.transpose(wb_bank(i)[:, k * P:(k + 1) * P], wb_rows[j][:, c:c + P], ident)
                mm.then_inc(wb_t, 1)

            def x_transposes(t):
                pe.wait_ge(x_twice, t + 1)
                if later(t, 1):
                    pe.wait_ge(v_ready, t)
                for r in range(2):
                    mm = pe.transpose(xps[:, r * P:(r + 1) * P], xd[:, r, :, :].rearrange("p d n -> p (d n)"), ident)
                mm.then_inc(w_ready, 1)

            def k_transposed(t):
                pe.wait_ge(v_ready, t + 1)
                pe.wait_ge(b_ready, t + 1)
                for h in range(HT):
                    mm = pe.matmul(turnp[:, h * P:(h + 1) * P], b_sb[:, h, :, :].rearrange("p x y -> p (x y)"),
                                   v_sb[:, h, :, :].rearrange("p a c -> p (a c)"), start=True, stop=True)
                mm.then_inc(kt_ready, 1)

            def k_rows(t):
                pe.wait_ge(kt_hi, t + 1)
                pe.wait_ge(kt_copied, t + 1)
                for k in range(KC):
                    mm = pe.transpose(turnp[:, k * P:(k + 1) * P], kt_full[:, k, :], ident)
                mm.then_inc(h1_ready, 1)

            def h2_transposes(t, par):
                pe.wait_ge(h2_ready, t + 1)
                for k in range(KC):
                    mm = pe.transpose(turnp[:, k * P:(k + 1) * P], h2[par][:, k * P:(k + 1) * P], ident)
                mm.then_inc(h2t_ready, 1)

            def product_part(acc, n, a, w, k, first, last):
                cols = acc[:, n * HALF:(n + 1) * HALF].rearrange("p (j n) -> p j n", n=P)
                rows = w[:, n * HK:(n + 1) * HK, k, :] if k is not None else \
                    w[:, n * HALF:(n + 1) * HALF].rearrange("p (j n) -> p j n", n=P)
                return pe.matmul(cols, a, rows, start=first, stop=last)

            def product(acc, hi, lo, w_hi, w_lo, k, first, last, halves=(0, 1)):
                for a, w in ((hi, w_hi), (hi, w_lo), (lo, w_hi)):
                    for n in halves:
                        mm = product_part(acc, n, a, w, k, first and a is hi and w is w_hi, last and a is lo)
                return mm

            def cat_means():
                pe.wait_ge(rt_copied, 1)
                pe.wait_ge(lora_in, 16 * KC)
                for k in range(KC):
                    mm = pe.matmul(small[:, 0:CAT], kst[:, K_MEAN:K_MEAN + P], cat_raw[:, k, :],
                                   start=k == 0, stop=k == KC - 1)
                mm.then_inc(cat_mean, 1)

            def first_attention(n, chunks):
                for k in chunks:
                    mm = product(acc_a, x1_hi[:, k, :], x1_lo[:, k, :], wa_hi, wa_lo, k, k == 0, k == KC - 1, (n,))
                    if n == 1 and k == KC - 1:
                        mm.then_inc(attn_ready, 1)
                    if n == 1 and k >= HK:
                        wb_half(k - HK)

            def lora_router(t):
                x_hi, x_lo = x2_of(t)
                for k in range(KC):
                    pe.matmul(small[:, 0:2 * CAT], x_hi[:, k, :], wr[:, k, :, :].rearrange("p s n -> p (s n)"),
                              start=k == 0, stop=False)
                    mm = pe.matmul(small[:, 0:CAT], x_lo[:, k, :], wr[:, k, 0, :], start=False, stop=k == KC - 1)
                mm.then_inc(cat_ready, 1)

            def gated_transpose(t):
                pe.wait_ge(hw_ready, t + 1)
                pe.transpose(small[:, 0:P], hw_sb[:, :, :].rearrange("p e r -> p (e r)"), ident).then_inc(hwt_ready, 1)

            def base(t, k, halves=(0, 1)):
                x_hi, x_lo = x2_of(t)
                product(acc_b, x_hi[:, k, :], x_lo[:, k, :], wb_hi, wb_lo, k, k == 0, False, halves)

            def experts(halves=(0, 1)):
                product(acc_b, hw_hi[:, :], hw_lo[:, :], lb_hi, lb_lo, None, False, True, halves).then_inc(ffn_ready, 1)

            def attention(t, k):
                mm = product(acc_a, x1_hi[:, k, :], x1_lo[:, k, :], wa_hi, wa_lo, k, k == 0, k == KC - 1)
                if k == KC - 1:
                    mm.then_inc(attn_ready, 1)

            def step(t, par):
                pe.wait_ge(h1_copied, t + 1)
                h2_transposes(t - 1, 1 - par)
                pe.wait_ge(kt_lo, t + 1)
                for k in range(KC):
                    attention(t, k)
                pe.wait_ge(h2t_lo, t)
                if real(t + 1):
                    k_transposed(t + 1)
                pe.wait_ge(hwt_lo, t - 1)
                lora_router(t - 1)
                pe.wait_ge(out_ready, t - 1)
                for k in range(KC):
                    if k == 2 and real(t + 2):
                        x_transposes(t + 2)
                    if k == KC // 2 and real(t + 1):
                        k_rows(t + 1)
                    if k == KC // 2 and at(t, TILES - 1):
                        h2_transposes(t, par)
                    if k == KC - 2:
                        gated_transpose(t - 1)
                    base(t - 1, k)
                pe.wait_ge(hwt_lo, t)
                experts()

            pe.wait_ge(consts_in, 16)
            x_transposes(0)
            block_sums(0)
            block_sums(1)
            wa_transposes(0)
            block_sums(2)
            wa_transposes(1)
            block_sums(3)
            wa_transposes(2)
            block_sums(4)
            wa_transposes(3)
            k_transposed(0)
            block_sums(5)
            wa_transposes(4)
            k_rows(0)
            block_sums(6)
            wa_transposes(5)
            block_sums(7)
            pe.wait_ge(kt_lo, 1)
            pe.wait_ge(wa_high, NWT)
            pe.wait_ge(wa_low, NWT // 2)
            first_attention(0, range(0, 1))
            wa_transposes(6)
            x_transposes(1)
            first_attention(0, range(1, 4))
            wa_transposes(7)
            first_attention(0, range(4, KC))
            pe.wait_ge(rt_in, 16)
            pe.transpose(small[:, HALF - rt_rows:HALF], rt_stage, ident[0:rt_rows, 0:rt_rows]).then_inc(rt_t, 1)
            pe.wait_ge(wa_high, 2 * NWT)
            pe.wait_ge(wa_low, DIRECT)
            pe.wait_ge(wa_low_direct, 2 * (NWT - DIRECT))
            first_attention(1, range(KC))
            pe.wait_ge(h1_copied, 1)
            k_transposed(1)
            wb_half(4)
            wb_half(5)
            x_transposes(2)
            k_rows(1)
            pe.wait_ge(h1_copied, 2)
            h2_transposes(0, 0)
            pe.wait_ge(kt_lo, 2)
            half = {2: 6, 3: 7, 5: 8, 6: 9}
            for k in range(KC):
                attention(1, k)
                if k in half:
                    wb_half(half[k])
            cat_means()
            wb_half(10)
            wb_half(11)
            pe.wait_ge(h2t_lo, 1)
            k_transposed(2)
            pe.wait_ge(wb_high, LATE)
            pe.wait_ge(wb_low, LATE)
            for k in range(KC):
                base(0, k, (0,))
                if k % 2:
                    wb_half(LATE + k // 2)
            pe.wait_ge(cat_lo, 1)
            lora_router(0)
            pe.wait_ge(wb_high, 2 * NWT)
            pe.wait_ge(wb_low, 2 * NWT)
            for k in range(KC):
                if k == 2:
                    x_transposes(3)
                if k == KC // 2:
                    k_rows(2)
                if k == KC - 2:
                    gated_transpose(0)
                base(0, k, (1,))
            pe.wait_ge(lorb_lo, 1)
            pe.wait_ge(hwt_lo, 1)
            experts()

            steps(pe, step)

            pe.wait_ge(h2t_lo, TILES)
            pe.wait_ge(hwt_lo, TILES - 1)
            lora_router(TILES - 1)
            pe.wait_ge(out_ready, TILES - 1)
            for k in range(KC):
                base(TILES - 1, k, (0,))
            for k in range(KC // 2):
                base(TILES - 1, k, (1,))
            gated_transpose(TILES - 1)
            for k in range(KC // 2, KC):
                base(TILES - 1, k, (1,))
            pe.wait_ge(hwt_lo, TILES)
            experts((0,))
            experts((1,))

        @block.scalar
        def _(act):
            def wa_centre(j):
                act.wait_ge(wa_masked, j + 1)
                act.activation(wa_neg[:, j:j + 1], wa_sum[:, j:j + 1], ACT.Copy, scale=-1.0 / L).then_inc(wa_mean, 1)
                act.wait_ge(wa_mean, j + 1)
                act.activation(wa_rows[j], wa_rows[j], ACT.Identity, bias=wa_neg[:, j:j + 1]).then_inc(wa_centred, 1)

            def wa_copies(j):
                for i in (2 * j, 2 * j + 1):
                    act.wait_ge(wa_t, i + 1)
                    act.activation(half_of(wa_hi, i), half_bank(i), ACT.Copy).then_inc(wa_high, 1)
                    if j < DIRECT:
                        act.activation(raw_half(i), half_bank(i), ACT.Copy).then_inc(wa_copied, 1)

            def wb_sums(j):
                act.wait_ge(wb_in[j], 16)
                act.activation(junk[:, :], wb_rows[j], ACT.Copy, accum_out=wb_sum[:, j:j + 1]).then_inc(wb_summed, 1)
                act.wait_ge(wb_summed, j + 1)
                act.activation(wb_neg[:, j:j + 1], wb_sum[:, j:j + 1], ACT.Copy, scale=-1.0 / L).then_inc(wb_mean, 1)

            def wb_highs(i):
                act.wait_ge(wb_t, i + 1)
                if i == 0:
                    act.wait_ge(mask_summed, NWT)
                act.activation(half_of(wb_hi, i), wb_bank(i), ACT.Copy).then_inc(wb_high, 1)

            def x_rows_twice(t):
                act.wait_ge(x_in, t * 16 + 16)
                if later(t, 1):
                    act.wait_ge(w_ready, t)
                for r in range(2):
                    op = act.activation(xd[:, r, :, :], xn[:, :, r].unsqueeze(1).to_broadcast([P, 2, N]), ACT.Copy)
                op.then_inc(x_twice, 1)

            def exp_and_sin(t):
                act.wait_ge(tab_exponent, t + 1)
                if later(t, 1):
                    act.wait_ge(b_ready, t)
                act.activation(er_t[:, :, :], er_t[:, :, :], ACT.Exp).then_inc(tab_exp, 1)
                act.wait_ge(tab_phase, t + 1)
                g_a, g_b0 = g_t[:, :, 0:NA], g_t[:, :, NA:NA + NB0]
                h_a, h_b0 = h_t[:, :, 0:NA], h_t[:, :, NA:NA + NB0]
                act.activation(xy[:, 0], g_a, ACT.Sin, scale=-TWO_PI, bias=col(COL_BX))
                act.activation(xy[:, 1], h_a, ACT.Sin, scale=col(COL_S), bias=col(COL_BY))
                act.activation(pp[:, 0], a_t[:, :, :], ACT.Sin, scale=-TWO_PI, bias=col(COL_HALF))
                act.activation(pp[:, 1], u_t[:, :, SB1], ACT.Sin, scale=col(COL_S))
                act.activation(qq[:, 0], g_b0, ACT.Sin, scale=col(COL_S), bias=col(COL_BX))
                act.activation(qq[:, 1], h_b0, ACT.Sin, scale=col(COL_NS), bias=col(COL_BQ))\
                    .then_inc(tab_sin, 1)

            def k_high(t):
                by_head = turnp[:, :].rearrange("p (h a c) -> p h a c", h=HT, a=NA)
                act.wait_ge(kt_ready, t + 1)
                act.activation(kt_full.rearrange("p a (h c) -> p h a c", c=C), by_head, ACT.Copy).then_inc(kt_copied, 1)
                if later(t, 1):
                    act.wait_ge(attn_ready, t)
                act.activation(x1_hi[:, :, :].rearrange("p a (h c) -> p h a c", c=C), by_head, ACT.Copy)\
                    .then_inc(kt_hi, 1)

            def deviation(s, src, stat, dev, t):
                act.activation(s[:, 1:2], s[:, 0:1], ACT.Copy, scale=-1.0 / L).then_inc(stat, 1)
                act.wait_ge(stat, t * 2 + 1)
                act.activation(junk[:, :], src, ACT.Square, bias=s[:, 1:2], accum_out=s[:, 2:3]).then_inc(stat, 1)
                act.wait_ge(stat, t * 2 + 2)
                act.activation(s[:, 3:4], s[:, 2:3], ACT.Sqrt, scale=1.0 / L, bias=col(COL_EPS)).then_inc(dev, 1)

            def h2_deviation(t, par):
                act.wait_ge(h2_ready, t + 1)
                deviation(st2[:, par, :], h2[par][:, :], h2_stat, h2_dev, t)

            def k_copy(t):
                act.wait_ge(h1_ready, t + 1)
                if later(t, 1):
                    act.wait_ge(h2_ready, t)
                act.activation(h1[:, :], turnp[:, :], ACT.Copy, accum_out=st1[:, 0:1]).then_inc(h1_copied, 1)

            def k_deviation(t):
                act.wait_ge(h1_copied, t + 1)
                deviation(st1, h1[:, :], h1_stat, h1_dev, t)

            def h2_high(t):
                act.wait_ge(h2t_ready, t + 1)
                act.activation(x2_of(t)[0][:, :, :].rearrange("p k n -> p (k n)"), turnp[:, :], ACT.Copy)\
                    .then_inc(h2t_hi, 1)

            def gated_high(t):
                act.wait_ge(hwt_ready, t + 1)
                act.activation(hw_hi[:, :], small[:, 0:P], ACT.Copy).then_inc(hwt_hi, 1)

            def step(t, par):
                act.wait_ge(ffn_ready, t - 1)
                h2_high(t - 1)
                if real(t + 2):
                    x_rows_twice(t + 2)
                    exp_and_sin(t + 2)
                if real(t + 1):
                    k_high(t + 1)
                h2_deviation(t, par)
                if real(t + 1):
                    k_copy(t + 1)
                    k_deviation(t + 1)
                gated_high(t - 1)

            act.wait_ge(consts_in, 16)
            act.wait_ge(pstep, P_ARGS)
            act.activation(slot[5], slot[1], ACT.Tanh, scale=0.5)
            act.activation(slot[6], slot[2], ACT.Sin, scale=TWO_PI)
            act.activation(slot[7], slot[2], ACT.Sin, scale=TWO_PI / 2).then_inc(halfstep, 1)
            x_rows_twice(0)
            exp_and_sin(0)
            wa_centre(0)
            wa_centre(1)
            wa_copies(0)
            wa_centre(2)
            wa_copies(1)
            wa_centre(3)
            wa_copies(2)
            wa_copies(3)
            exp_and_sin(1)
            wa_centre(4)
            k_high(0)
            x_rows_twice(1)
            wa_copies(4)
            wa_copies(5)
            k_copy(0)
            k_deviation(0)
            wa_copies(6)
            wb_sums(0)
            wa_copies(7)
            wb_sums(1)
            x_rows_twice(2)
            wb_sums(2)
            wb_sums(3)
            wb_sums(4)
            wb_highs(0)
            wb_highs(1)
            wb_highs(2)
            wb_sums(5)
            wb_highs(3)
            k_high(1)
            wb_highs(4)
            wb_highs(5)
            k_copy(1)
            wb_sums(6)
            h2_high(0)
            wb_sums(7)
            exp_and_sin(2)
            wb_highs(6)
            wb_highs(7)
            wb_highs(8)
            wb_highs(9)
            k_deviation(1)
            wb_highs(10)
            wb_highs(11)
            h2_deviation(0, 0)
            k_high(2)
            act.wait_ge(cat_centred, 1)
            act.activation(wr[:, :, 0, :], cat_raw, ACT.Copy).then_inc(cat_hi, 1)
            for i in range(LATE, 2 * NWT):
                wb_highs(i)
            act.wait_ge(lorb_in, 16)
            act.activation(lb_hi[:, :], lb_raw[:, :], ACT.Copy).then_inc(lorb_hi, 1)
            x_rows_twice(3)
            exp_and_sin(3)
            k_copy(2)
            gated_high(0)
            h2_deviation(1, 1)
            k_deviation(2)

            steps(act, step)

            act.wait_ge(attn_ready, TILES)
            h2_high(TILES - 1)
            gated_high(TILES - 1)

        @block.gpsimd
        def _(pool):
            def parameters():
                n = 0

                def link(op):
                    nonlocal n
                    op.then_inc(qstep, 1)
                    n += 1
                    pool.wait_ge(qstep, n)

                pool.wait_ge(pstep, P_ARGS)
                two = lambda s: s.rearrange("p (s h) -> p s h", s=2)
                lr, li = lam_sb[:, 0:1], lam_sb[:, 1:2]
                pool.wait_ge(halfstep, 1)
                th, s_, sh = slot[5], slot[6], slot[7]
                link(pool.tensor_tensor(sh, sh, sh, ALU.mult))
                pool.tensor_scalar(slot[0], sh, -2.0, 1.0, ALU.mult, ALU.add)
                link(pool.tensor_scalar(sh, sh, 2.0, None, ALU.mult))
                pool.wait_ge(q_reciprocal, 1)
                link(pool.tensor_tensor(th, th, slot[3], ALU.mult))
                pool.tensor_scalar(slot[1], th, 1.0, None, ALU.add)
                link(pool.tensor_tensor(slot[3], th, slot[0], ALU.mult))
                pool.tensor_tensor(slot[3], slot[3], sh, ALU.subtract)
                link(pool.tensor_tensor(s_, slot[1], s_, ALU.mult))
                nr, dr, ni, di = two(slot[3])[:, 0], two(slot[3])[:, 1], two(s_)[:, 0], two(s_)[:, 1]
                d_r, d_i = two(slot[4])[:, 0], two(slot[4])[:, 1]
                w0, w1 = two(slot[0])[:, 0], two(slot[0])[:, 1]
                pool.tensor_scalar(w0, di, li, None, ALU.mult)
                pool.tensor_scalar(w1, di, lr, None, ALU.mult)
                pool.tensor_scalar(d_r, dr, lr, None, ALU.mult)
                link(pool.tensor_scalar(d_i, dr, li, None, ALU.mult))
                pool.tensor_tensor(d_r, d_r, w0, ALU.subtract)
                link(pool.tensor_tensor(d_i, d_i, w1, ALU.add))
                m0, m1 = two(slot[1])[:, 0], two(slot[1])[:, 1]
                pool.tensor_tensor(m0, d_r, d_r, ALU.mult)
                link(pool.tensor_tensor(m1, d_i, d_i, ALU.mult))
                link(pool.tensor_tensor(m0, m0, m1, ALU.add))
                link(pool.tensor_scalar(m0, m0, REC_EPS, None, ALU.add))
                a0, a1 = two(slot[2])[:, 0], two(slot[2])[:, 1]
                b0, b1 = two(slot[5])[:, 0], two(slot[5])[:, 1]
                pool.tensor_tensor(a0, nr, d_r, ALU.mult)
                pool.tensor_tensor(a1, ni, d_i, ALU.mult)
                pool.tensor_tensor(b0, ni, d_r, ALU.mult)
                link(pool.tensor_tensor(b1, nr, d_i, ALU.mult))
                pool.tensor_tensor(a0, a0, a1, ALU.add)
                link(pool.tensor_tensor(b0, b0, b1, ALU.subtract))
                pool.wait_ge(q_reciprocal, 2)
                pool.tensor_tensor(qr[:, :], a0, m1, ALU.mult)
                pool.tensor_tensor(qi[:, :], b0, m1, ALU.mult).then_inc(q_ready, 1)

            def table_b(t):
                pool.wait_ge(b_chain, t * 3 + 1)
                if t == 0:
                    pool.wait_ge(q_ready, 1)
                else:
                    pool.wait_ge(h1_ready, t)
                    pool.wait_ge(kt_lo, t)
                pool.tensor_tensor(whole(b_sb), *b_factors(0), ALU.mult).then_inc(b_chain, 1)
                pool.tensor_tensor(b_terms(h2[1]), *b_factors(1), ALU.mult).then_inc(b_chain, 1)
                pool.wait_ge(b_chain, t * 3 + 3)
                pool.tensor_tensor(whole(b_sb), whole(b_sb), b_terms(h2[1]), ALU.add).then_inc(b_ready, 1)

            def wa_centre(j):
                pool.wait_ge(wa_masked, j + 1)
                pool.tensor_scalar(wa_neg[:, j:j + 1], wa_sum[:, j:j + 1], -1.0 / L, 0.0, ALU.mult, ALU.add)\
                    .then_inc(wa_mean_last, 1)
                pool.wait_ge(wa_mean_last, j + 1 - CENTRE_LAST)
                pool.tensor_scalar(wa_rows[j], wa_rows[j], 1.0, wa_neg[:, j:j + 1], ALU.mult, ALU.add)\
                    .then_inc(wa_centred_last, 1)

            def wa_lows(j):
                pool.wait_ge(wa_copied, 2 * j + 2)
                pool.tensor_tensor(wa_lo[:, j], wa_rows[j].rearrange("p (k n) -> p k n", n=P), wa_hi[:, j].bitcast(F),
                                   ALU.subtract).then_inc(wa_low, 1)

            def wb_centre(j):
                pool.wait_ge(wb_mean, j + 1)
                pool.tensor_scalar(wb_rows[j], wb_rows[j], 1.0, wb_neg[:, j:j + 1], ALU.mult, ALU.add)\
                    .then_inc(wb_centred, 1)

            parameters()
            table_b(0)
            wa_lows(0)
            wa_lows(1)
            wa_centre(5)
            wa_lows(2)
            wa_lows(3)
            wa_centre(6)
            wa_centre(7)
            table_b(1)
            for j in range(NWT):
                wb_centre(j)
            table_b(2)
            pool.wait_ge(cat_hi, 1)
            pool.tensor_tensor(wr[:, :, 1, :], cat_raw, wr[:, :, 0, :].bitcast(F), ALU.subtract).then_inc(cat_lo, 1)
            pool.wait_ge(lorb_hi, 1)
            pool.tensor_tensor(lb_lo[:, :], lb_raw[:, :], lb_hi[:, :].bitcast(F), ALU.subtract).then_inc(lorb_lo, 1)

            def add_bias(t, par):
                pool.wait_ge(h2t_ready, t + 1)
                pool.wait_ge(h2_dev, t + 1)
                pool.tensor_tensor(h2[par][:, :], h2[par][:, :], bias[:, :], ALU.add).then_inc(bias_added, 1)

            def step(t, par):
                add_bias(t - 1, 1 - par)

            pool.wait_ge(bias_in, 32)
            add_bias(0, 0)
            steps(pool, step)
            add_bias(TILES - 1, 1)

        @block.vector
        def _(dve):
            def chained(s, base):
                n = [base]

                def link(op):
                    op.then_inc(s, 1)
                    n[0] = n[0] + 1
                    dve.wait_ge(s, n[0])
                return link

            def dve_arguments():
                link = chained(pstep, 0)
                x_, k_, r_, p_, w_ = slot[4], slot[0], slot[1], slot[2], slot[3]
                link(dve.tensor_scalar(k_, x_, LOG2E, ROUND, ALU.mult, ALU.add))
                link(dve.tensor_scalar(k_, k_, ROUND, None, ALU.subtract))
                link(dve.tensor_scalar(k_, k_, -126.0, 127.0, ALU.max, ALU.min))
                link(dve.scalar_tensor_tensor(r_, k_, -LN2_HI, x_, ALU.mult, ALU.add))
                link(dve.scalar_tensor_tensor(r_, k_, -LN2_LO, r_, ALU.mult, ALU.add))
                link(dve.tensor_scalar(w_.bitcast(I32), k_, 127.0, 8388608.0, ALU.add, ALU.mult))
                link(dve.tensor_scalar(p_, r_, 1.0 / 5040, None, ALU.mult))
                for c in (1.0 / 720, 1.0 / 120, 1.0 / 24, 1.0 / 6, 0.5, 1.0):
                    link(dve.scalar_tensor_tensor(p_, p_, c, r_, ALU.add, ALU.mult))
                link(dve.scalar_tensor_tensor(p_, p_, 1.0, w_, ALU.add, ALU.mult))
                dt = p_.rearrange("p (h r) -> p r h", r=2)
                lr, li = lam_sb[:, 0:1], lam_sb[:, 1:2]
                dve.tensor_scalar(dec[:, :], dt[:, 0, :], lr, None, ALU.mult)
                dve.tensor_scalar(gt[:, :], lr, 0.0, None, ALU.is_gt)
                link(dve.tensor_scalar(turn[:, :], dt[:, 1, :], li, None, ALU.mult))
                dve.tensor_scalar(neg_gt[:, :], gt[:, :], -1.0, None, ALU.mult)
                dve.tensor_scalar(flip[:, :], gt[:, :], -2.0, 1.0, ALU.mult, ALU.add)
                link(dve.tensor_scalar(turn[:, :], turn[:, :], INV_TWO_PI, None, ALU.mult))
                dve.scalar_tensor_tensor(mul[:, :], kst[:, K_OFF:K_OFF + NM], neg_gt[:, 0:1], kst[:, K_MUL:K_MUL + NM],
                                         ALU.mult, ALU.add)
                two = lambda s: s.rearrange("p (s h) -> p s h", s=2)
                a_, f_ = slot[1], slot[2]
                dve.tensor_scalar(two(a_)[:, 0], dec[:, :], flip[:, 0:1], None, ALU.mult)
                link(dve.tensor_scalar(two(f_)[:, 0], turn[:, :], flip[:, 0:1], None, ALU.mult))
                dve.tensor_scalar(two(a_)[:, 1], two(a_)[:, 0], float(L), None, ALU.mult)
                link(dve.tensor_scalar(two(f_)[:, 1], two(f_)[:, 0], float(L), None, ALU.mult))
                link(dve.tensor_scalar(slot[3], f_, ROUND, -ROUND, ALU.add, ALU.add))
                link(dve.tensor_tensor(f_, f_, slot[3], ALU.subtract))

            def reciprocal_of_tanh():
                dve.wait_ge(halfstep, 1)
                dve.tensor_scalar(slot[3], slot[5], -0.5, 0.5, ALU.mult, ALU.add).then_inc(pstep, 1)
                dve.wait_ge(pstep, P_ARGS + 1)
                dve.reciprocal(slot[3], slot[3]).then_inc(q_reciprocal, 1)

            def reciprocal_of_norm():
                dve.wait_ge(qstep, Q_NORM)
                dve.reciprocal(slot[1][:, H:2 * H], slot[1][:, 0:H]).then_inc(q_reciprocal, 1)

            def mask_sums(j):
                dve.wait_ge(mask_in[j], 16)
                dve.tensor_reduce(mask_sum[:, j, :], mask_rows[j].rearrange("p (k b) -> p k b", b=32), AX.X, ALU.add)\
                    .then_inc(mask_summed, 1)

            def wa_mask(j):
                dve.wait_ge(blk_ready, j + 1)
                dve.wait_ge(wa_in[j], 16)
                blocks = block_bank(j).unsqueeze(2).to_broadcast([P, L // 32, 32])
                rows = wa_rows[j].rearrange("p (k b) -> p k b", b=32)
                dve.scalar_tensor_tensor(rows, blocks, 0.0, rows, ALU.is_gt, ALU.mult, accum_out=wa_sum[:, j:j + 1])\
                    .then_inc(wa_masked, 1)

            def wa_lows(i):
                dve.wait_ge(wa_high, i + 1)
                dve.tensor_tensor(half_of(wa_lo, i), half_bank(i), half_of(wa_hi, i).bitcast(F), ALU.subtract)\
                    .then_inc(wa_low_direct, 1)

            def wb_lows(i):
                dve.wait_ge(wb_high, i + 1)
                dve.wait_ge(wb_t, i + 1)
                dve.tensor_tensor(half_of(wb_lo, i), wb_bank(i), half_of(wb_hi, i).bitcast(F), ALU.subtract)\
                    .then_inc(wb_low, 1)

            def over_j(v, n):
                return v.unsqueeze(2).to_broadcast([P, HT, n])

            def decay(s, n):
                return er_t[:, :, s].unsqueeze(1).to_broadcast([P, 2, HT, n])

            def phases(t):
                link = chained(tab_chain, t * 3)
                heads = bass.ds(t * HT, HT)
                m = mul[:, :].unsqueeze(1).to_broadcast([P, HT, NM])
                dve.tensor_tensor(er_t[:, :, :], over_j(dec[:, heads], NM), m, ALU.mult).then_inc(tab_exponent, 1)
                link(dve.tensor_tensor(u_t[:, :, :], over_j(turn[:, heads], NM), m, ALU.mult))
                link(dve.tensor_scalar(k_t, u_t[:, :, :], ROUND, -ROUND, ALU.add, ALU.add))
                link(dve.tensor_tensor(u_t[:, :, :], u_t[:, :, :], k_t, ALU.subtract))
                ab = u_t[:, :, 0:NA + NB0]
                dve.scalar_tensor_tensor(g_t, ab, col(COL_G), ab, ALU.mult, ALU.max)
                dve.scalar_tensor_tensor(h_t, ab, col(COL_H), ab, ALU.mult, ALU.max)
                dve.scalar_tensor_tensor(a_t[:, :, :], u_t[:, :, SB1], -1.0, u_t[:, :, SB1], ALU.mult, ALU.max)\
                    .then_inc(tab_phase, 1)

            def table_v(t):
                heads = bass.ds(t * HT, HT)

                def q(v):
                    return v[:, heads].unsqueeze(1).unsqueeze(3).to_broadcast([P, 2, HT, NA])

                def w(r):
                    rows = xps[:, r * P:(r + 1) * P].rearrange("p (h c) -> p h c", c=C)
                    return rows.unsqueeze(2).to_broadcast([P, HT, NA, C])

                def u(i):
                    return u12[:, i].unsqueeze(3).to_broadcast([P, HT, NA, C])

                tmp4 = tmp[:, :].rearrange("p (h a c) -> p h a c", h=HT, a=NA)
                dve.wait_ge(tab_sin, t + 1)
                dve.tensor_tensor(whole(xy), whole(xy), decay(SA, NA), ALU.mult).then_inc(v_chain, 1)
                dve.wait_ge(v_chain, t * 4 + 1)
                dve.tensor_tensor(whole(t1), whole(xy), q(qr), ALU.mult)
                dve.tensor_tensor(whole(t2), whole(xy), q(qi), ALU.mult).then_inc(v_chain, 1)
                dve.wait_ge(v_chain, t * 4 + 2)
                dve.tensor_tensor(u12[:, 0], t1[:, 0], t2[:, 1], ALU.add)
                dve.tensor_tensor(u12[:, 1], t1[:, 1], t2[:, 0], ALU.subtract).then_inc(v_chain, 1)
                dve.wait_ge(w_ready, t + 1)
                if later(t, 1):
                    dve.wait_ge(kt_ready, t)
                    dve.wait_ge(b_ready, t)
                dve.wait_ge(v_chain, t * 4 + 3)
                dve.tensor_tensor(whole(v_sb), w(0), u(0), ALU.mult)
                dve.tensor_tensor(tmp4, w(1), u(1), ALU.mult).then_inc(v_chain, 1)
                dve.wait_ge(v_chain, t * 4 + 4)
                dve.tensor_tensor(whole(v_sb), whole(v_sb), tmp4, ALU.add).then_inc(v_ready, 1)

            def decay_b(t):
                dve.wait_ge(tab_sin, t + 1)
                dve.tensor_tensor(whole(pp), whole(pp), decay(SB1, NB1), ALU.mult)
                dve.tensor_tensor(whole(qq), whole(qq), decay(SB0, NB0), ALU.mult).then_inc(b_chain, 1)

            def table_b(t):
                decay_b(t)
                dve.wait_ge(h1_ready, t)
                dve.wait_ge(kt_lo, t)
                dve.wait_ge(v_ready, t + 1)
                dve.wait_ge(b_chain, t * 3 + 1)
                dve.tensor_tensor(whole(b_sb), *b_factors(0), ALU.mult)
                dve.tensor_tensor(b_terms(tmp), *b_factors(1), ALU.mult).then_inc(b_chain, 2)
                dve.wait_ge(b_chain, t * 3 + 3)
                dve.tensor_tensor(whole(b_sb), whole(b_sb), b_terms(tmp), ALU.add).then_inc(b_ready, 1)

            def k_low(t):
                dve.wait_ge(kt_copied, t + 1)
                dve.wait_ge(kt_hi, t + 1)
                dve.tensor_tensor(x1_lo[:, :, :], kt_full, x1_hi[:, :, :].bitcast(F), ALU.subtract).then_inc(kt_lo, 1)

            def reciprocal_deviation(s, dev, s_chain, t):
                dve.wait_ge(dev, t + 1)
                dve.tensor_scalar(s[:, 4:5], s[:, 2:3], 1.0 / L, LN_EPS, ALU.mult, ALU.add)
                dve.reciprocal(s[:, 5:6], s[:, 3:4]).then_inc(s_chain, 1)
                dve.wait_ge(s_chain, t * 4 + 1)
                dve.scalar_tensor_tensor(s[:, 6:7], s[:, 5:6], s[:, 5:6], s[:, 4:5], ALU.mult, ALU.mult).then_inc(s_chain, 1)
                dve.wait_ge(s_chain, t * 4 + 2)
                dve.tensor_scalar(s[:, 7:8], s[:, 6:7], -0.5, 1.5, ALU.mult, ALU.add).then_inc(s_chain, 1)
                dve.wait_ge(s_chain, t * 4 + 3)
                dve.tensor_tensor(s[:, 4:5], s[:, 5:6], s[:, 7:8], ALU.mult).then_inc(s_chain, 1)

            def attention_residual(t, par):
                dve.wait_ge(attn_ready, t + 1)
                dve.wait_ge(rs1_chain, t * 4 + 4)
                dve.scalar_tensor_tensor(h2[par][:, :], acc_a[:, :], st1[:, 4:5], h1[:, :], ALU.mult, ALU.add,
                                         accum_out=st2[:, par, 0:1]).then_inc(h2_ready, 1)

            def gates(t, par):
                link = chained(gate_chain, t * 9)
                z, cnt, tot, inv, cand, w = (gs[:, i, :] for i in range(6))
                z_j = z.unsqueeze(1).to_broadcast([P, E, E])
                z_i = z.unsqueeze(2).to_broadcast([P, E, E])
                dve.wait_ge(cat_ready, t + 1)
                dve.wait_ge(rs2_chain, t * 4 + 4)
                link(dve.tensor_copy(cat[:, :], small[:, CAT:2 * CAT]))
                link(dve.tensor_tensor(cat[:, :], small[:, 0:CAT], cat[:, :], ALU.add))
                link(dve.scalar_tensor_tensor(z, cat[:, E * R:CAT], st2[:, par, 4:5], bias_r[:, :], ALU.mult, ALU.add))
                link(dve.tensor_tensor(gate[:, 0], z_j, z_i, ALU.is_ge))
                dve.tensor_reduce(cnt, gate[:, 0], AX.X, ALU.add)
                link(dve.tensor_tensor(gate[:, 1], gate[:, 0], z_j, ALU.mult))
                dve.reciprocal(inv, cnt)
                link(dve.tensor_reduce(tot, gate[:, 1], AX.X, ALU.add))
                link(dve.scalar_tensor_tensor(cand, tot, -1.0, inv, ALU.add, ALU.mult))
                link(dve.tensor_reduce(tau[:, :], cand, AX.X, ALU.max))
                link(dve.tensor_scalar(w, z, tau[:, 0:1], 0.0, ALU.subtract, ALU.max))
                dve.tensor_tensor(hw_sb[:, :, :], cat[:, 0:E * R].rearrange("p (e r) -> p e r", e=E),
                                  w.unsqueeze(2).to_broadcast([P, E, R]), ALU.mult).then_inc(hw_ready, 1)

            def h2_low(t):
                dve.wait_ge(h2t_hi, t + 1)
                hi, lo = x2_of(t)
                dve.tensor_tensor(lo[:, :, :].rearrange("p k n -> p (k n)"), turnp[:, :],
                                  hi[:, :, :].bitcast(F).rearrange("p k n -> p (k n)"), ALU.subtract)\
                    .then_inc(h2t_lo, 1)

            def gated_low(t):
                dve.wait_ge(hwt_hi, t + 1)
                dve.tensor_tensor(hw_lo[:, :], small[:, 0:P], hw_hi[:, :].bitcast(F), ALU.subtract).then_inc(hwt_lo, 1)

            def result(t, par, cols=slice(0, L)):
                dve.wait_ge(bias_added, t + 1)
                h = h2[par][:, cols]
                dve.scalar_tensor_tensor(h, acc_b[:, cols], st2[:, par, 4:5], h, ALU.mult, ALU.add).then_inc(out_ready, 1)

            def h1_reciprocal(t):
                reciprocal_deviation(st1, h1_dev, rs1_chain, t)

            def h2_reciprocal(t, par):
                reciprocal_deviation(st2[:, par, :], h2_dev, rs2_chain, t)

            def step(t, par):
                h2_low(t - 1)
                h2_reciprocal(t - 1, 1 - par)
                h1_reciprocal(t)
                if real(t + 1):
                    table_b(t + 1)
                if real(t + 2):
                    phases(t + 2)
                dve.wait_ge(out_stored[par], t * 8 - 8 * par)
                attention_residual(t, par)
                if real(t + 1):
                    k_low(t + 1)
                gates(t - 1, 1 - par)
                if real(t + 2):
                    table_v(t + 2)
                gated_low(t - 1)
                if at(t, TILES - 1):
                    h2_low(t)
                dve.wait_ge(ffn_ready, t)
                result(t - 1, 1 - par)

            dve.wait_ge(params_in, 48)
            dve.wait_ge(consts_in, 16)
            dve_arguments()
            phases(0)
            mask_sums(0)
            reciprocal_of_tanh()
            mask_sums(1)
            wa_mask(0)
            mask_sums(2)
            wa_mask(1)
            mask_sums(3)
            wa_mask(2)
            decay_b(0)
            reciprocal_of_norm()
            mask_sums(4)
            wa_mask(3)
            dve.wait_ge(q_ready, 1)
            table_v(0)
            phases(1)
            mask_sums(5)
            wa_mask(4)
            mask_sums(6)
            wa_mask(5)
            decay_b(1)
            k_low(0)
            wa_lows(8)
            wa_lows(9)
            mask_sums(7)
            wa_mask(6)
            wa_lows(10)
            wa_lows(11)
            wa_mask(7)
            for i in range(12, 2 * NWT):
                wa_lows(i)
            table_v(1)
            dve.wait_ge(rt_t, 1)
            dve.tensor_copy(cat_raw[:, :, E * R:CAT],
                            small[:, HALF - rt_rows:HALF].rearrange("p (e k) -> p k e", e=E)).then_inc(rt_copied, 1)
            for i in range(4):
                wb_lows(i)
            h1_reciprocal(0)
            attention_residual(0, 0)
            k_low(1)
            phases(2)
            wb_lows(4)
            wb_lows(5)
            h2_low(0)
            decay_b(2)
            wb_lows(6)
            wb_lows(7)
            table_v(2)
            wb_lows(8)
            wb_lows(9)
            h1_reciprocal(1)
            wb_lows(10)
            wb_lows(11)
            dve.wait_ge(b_ready, 3)
            attention_residual(1, 1)
            dve.wait_ge(cat_mean, 1)
            dve.tensor_tensor(cat_raw, cat_raw, small[:, 0:CAT].unsqueeze(1).to_broadcast([P, KC, CAT]),
                              ALU.subtract).then_inc(cat_centred, 1)
            for i in range(LATE, LATE + 3):
                wb_lows(i)
            phases(3)
            wb_lows(LATE + 3)
            dve.wait_ge(bias_in, 32)
            h2_reciprocal(0, 0)
            k_low(2)
            gates(0, 0)
            gated_low(0)
            table_v(3)
            dve.wait_ge(ffn_ready, 1)
            result(0, 0)

            steps(dve, step)

            h2_reciprocal(TILES - 1, 1)
            gates(TILES - 1, 1)
            gated_low(TILES - 1)
            for n in range(2):
                dve.wait_ge(ffn_ready, TILES + n)
                result(TILES - 1, 1, slice(n * HALF, (n + 1) * HALF))


_INS = ['x', 'L0_tok_log_dt', 'L0_tok_Lambda', 'L0_attn_weight', 'L0_attn_mask', 'L0_ffn_W_base', 'L0_ffn_b_base',
        'L0_ffn_W_router', 'L0_ffn_b_router', 'L0_ffn_lora_A', 'L0_ffn_lora_B']


def kernel(**inputs):
    import numpy as _np
    import concourse.bacc as _bacc
    from concourse import mybir as _mybir
    from concourse.bass_utils import run_bass_kernel_spmd as _run

    nc = _bacc.Bacc("TRN2", target_bir_lowering=False, num_devices=1)
    arrays, args = {}, []
    for name in _INS:
        arrays[f"in_{name}"] = _np.ascontiguousarray(inputs[name])
    arrays["in_consts"] = constants()
    for name, a in arrays.items():
        args.append(nc.dram_tensor(name, a.shape, _mybir.dt.from_np(a.dtype), kind="ExternalInput").ap())
    out = nc.dram_tensor("out", (C, H, L), _mybir.dt.float32, kind="ExternalOutput").ap()
    build_vit_tower(nc, *args, out)
    return _run(nc, [arrays], core_ids=[0]).results[0]["out"]
```
